# Optimizing a Trainium2 kernel written in Bass

```python
import numpy as np
import jax
import jax.numpy as jnp

def _softmax(x, axis=-1):
    return jax.nn.softmax(x, axis=axis)

def _gelu(x):
    return jax.nn.gelu(x, approximate=True)

def _silu(x):
    return jax.nn.silu(x)

def _sigmoid(x):
    return jax.nn.sigmoid(x)

def _layernorm(x, axis=-1, eps=1e-05):
    m = jnp.mean(x, axis=axis, keepdims=True)
    v = jnp.var(x, axis=axis, keepdims=True)
    return (x - m) / jnp.sqrt(v + eps)

def _scatter_add(tgt, idx, src, axis=0):
    return tgt.at[idx].add(src)

def _segment_sum(src, seg, n):
    return jax.ops.segment_sum(src, seg, n)
kernel_name = 'mk_conv_seq_d2_conv_nchw512_r4_6c5825'

def setup_inputs(seed: int=0):
    np.random.seed(seed)
    _w = jnp.asarray

    def _rec_inputs():
        import jax
        import jax.numpy as jnp
        _gk = jax.random.key(seed)
        x = -0.0003929 + 0.9999 * jax.random.normal(jax.random.fold_in(_gk, 1), (32, 128, 32, 32), jnp.float32)
        return x
    x = _rec_inputs()

    def _L0_conv_setup():
        import jax, jax.numpy as jnp
        import numpy as np
        GROUPS = 32
        EPS = 1e-05

        def _group_norm(x, w, b):
            B, C, H, W = x.shape
            xg = x.reshape(B, GROUPS, C // GROUPS, H, W)
            mean = xg.mean(axis=(2, 3, 4), keepdims=True)
            var = xg.var(axis=(2, 3, 4), keepdims=True)
            xg = (xg - mean) * jax.lax.rsqrt(var + EPS)
            return xg.reshape(B, C, H, W) * w[None, :, None, None] + b[None, :, None, None]
        key = jax.random.key(seed)
        ks = jax.random.split(key, 7)
        B, C, H, W = (32, 128, 32, 32)
        x = jax.random.normal(ks[0], (B, C, H, W), dtype=jnp.float32)
        gn_w = jnp.ones((C,), dtype=jnp.float32)
        gn_b = jnp.zeros((C,), dtype=jnp.float32)
        qkv_w = jax.random.normal(ks[1], (3 * C, C), dtype=jnp.float32) * C ** (-0.5)
        qkv_b = jax.random.normal(ks[2], (3 * C,), dtype=jnp.float32) * 0.02
        proj_w = jax.random.normal(ks[3], (C, C), dtype=jnp.float32) * C ** (-0.5)
        proj_b = jax.random.normal(ks[4], (C,), dtype=jnp.float32) * 0.02
        return {'x': x, 'gn_w': gn_w, 'gn_b': gn_b, 'qkv_w': qkv_w, 'qkv_b': qkv_b, 'proj_w': proj_w, 'proj_b': proj_b}
    _L0_conv_all = _L0_conv_setup()
    _L0_conv_in = {k: v for k, v in _L0_conv_all.items() if k in ('gn_w', 'gn_b', 'qkv_w', 'qkv_b', 'proj_w', 'proj_b')}
    del _L0_conv_all

    def _L1_conv_setup():
        import jax, jax.numpy as jnp
        import numpy as np
        B, C, H, W = (4, 128, 16, 16)
        CQK = C // 8
        key = jax.random.key(seed)
        ks = jax.random.split(key, 8)
        s = 0.05
        return {'x': jax.random.normal(ks[0], (B, C, H, W), dtype=jnp.float32), 'Wq': jax.random.normal(ks[1], (CQK, C), dtype=jnp.float32) * s, 'bq': jax.random.normal(ks[2], (CQK,), dtype=jnp.float32) * s, 'Wk': jax.random.normal(ks[3], (CQK, C), dtype=jnp.float32) * s, 'bk': jax.random.normal(ks[4], (CQK,), dtype=jnp.float32) * s, 'Wv': jax.random.normal(ks[5], (C, C), dtype=jnp.float32) * s, 'bv': jax.random.normal(ks[6], (C,), dtype=jnp.float32) * s, 'gamma': jax.random.normal(ks[7], (1,), dtype=jnp.float32)}
    _L1_conv_all = _L1_conv_setup()
    _L1_conv_in = {k: v for k, v in _L1_conv_all.items() if k in ('Wq', 'bq', 'Wk', 'bk', 'Wv', 'bv', 'gamma')}
    del _L1_conv_all
    return {'x': x, 'L0_conv_gn_w': _L0_conv_in['gn_w'], 'L0_conv_gn_b': _L0_conv_in['gn_b'], 'L0_conv_qkv_w': _L0_conv_in['qkv_w'], 'L0_conv_qkv_b': _L0_conv_in['qkv_b'], 'L0_conv_proj_w': _L0_conv_in['proj_w'], 'L0_conv_proj_b': _L0_conv_in['proj_b'], 'L1_conv_Wq': _L1_conv_in['Wq'], 'L1_conv_bq': _L1_conv_in['bq'], 'L1_conv_Wk': _L1_conv_in['Wk'], 'L1_conv_bk': _L1_conv_in['bk'], 'L1_conv_Wv': _L1_conv_in['Wv'], 'L1_conv_bv': _L1_conv_in['bv'], 'L1_conv_gamma': _L1_conv_in['gamma']}

def reference(x, L0_conv_gn_w, L0_conv_gn_b, L0_conv_qkv_w, L0_conv_qkv_b, L0_conv_proj_w, L0_conv_proj_b, L1_conv_Wq, L1_conv_bq, L1_conv_Wk, L1_conv_bk, L1_conv_Wv, L1_conv_bv, L1_conv_gamma):
    import jax
    import jax.numpy as jnp

    def _L0_conv_ref(x, gn_w, gn_b, qkv_w, qkv_b, proj_w, proj_b):
        import jax, jax.numpy as jnp
        import numpy as np
        GROUPS = 32
        EPS = 1e-05

        def _group_norm(x, w, b):
            B, C, H, W = x.shape
            xg = x.reshape(B, GROUPS, C // GROUPS, H, W)
            mean = xg.mean(axis=(2, 3, 4), keepdims=True)
            var = xg.var(axis=(2, 3, 4), keepdims=True)
            xg = (xg - mean) * jax.lax.rsqrt(var + EPS)
            return xg.reshape(B, C, H, W) * w[None, :, None, None] + b[None, :, None, None]
        B, C, H, W = x.shape
        h = _group_norm(x, gn_w, gn_b).reshape(B, C, H * W)
        qkv = jnp.einsum('oc,bcn->bon', qkv_w, h) + qkv_b[None, :, None]
        q, k, v = jnp.split(qkv, 3, axis=1)
        scale = C ** (-0.5)
        attn = jax.nn.softmax(jnp.einsum('bcn,bcm->bnm', q, k) * scale, axis=-1)
        h = jnp.einsum('bcm,bnm->bcn', v, attn)
        h = jnp.einsum('oc,bcn->bon', proj_w, h) + proj_b[None, :, None]
        return x + h.reshape(B, C, H, W)

    def _L1_conv_ref(x, Wq, bq, Wk, bk, Wv, bv, gamma):
        import jax, jax.numpy as jnp
        import numpy as np
        B, C, H, W = (4, 128, 16, 16)
        CQK = C // 8
        b, c, h, w = x.shape
        hw = h * w
        q = jnp.einsum('bchw,dc->bdhw', x, Wq) + bq[None, :, None, None]
        k = jnp.einsum('bchw,dc->bdhw', x, Wk) + bk[None, :, None, None]
        v = jnp.einsum('bchw,dc->bdhw', x, Wv) + bv[None, :, None, None]
        q = q.reshape(b, -1, hw)
        k = k.reshape(b, -1, hw)
        v = v.reshape(b, -1, hw)
        attn = jax.nn.softmax(jnp.einsum('bdi,bdj->bij', q, k), axis=-1)
        out = jnp.einsum('bcj,bij->bci', v, attn).reshape(b, c, h, w)
        return gamma[0] * out + x

    def _gn(v, G=32, eps=1e-05):
        B_, C_, H_, W_ = v.shape
        g = v.reshape(B_, G, C_ // G, H_, W_)
        m = jnp.mean(g, axis=(2, 3, 4), keepdims=True)
        s = jnp.var(g, axis=(2, 3, 4), keepdims=True)
        return ((g - m) / jnp.sqrt(s + eps)).reshape(v.shape)

    def _ln_c(v, eps=1e-06):
        m = jnp.mean(v, axis=1, keepdims=True)
        s = jnp.var(v, axis=1, keepdims=True)
        return (v - m) / jnp.sqrt(s + eps)

    def _ln_t(v, eps=1e-05):
        m = jnp.mean(v, axis=-1, keepdims=True)
        s = jnp.var(v, axis=-1, keepdims=True)
        return (v - m) / jnp.sqrt(s + eps)

    def _to_tokens(v):
        B_, C_, H_, W_ = v.shape
        return v.reshape(B_, C_, H_ * W_).transpose(0, 2, 1)

    def _from_tokens(t, like):
        B_, C_, H_, W_ = like.shape
        return t.transpose(0, 2, 1).reshape(B_, C_, H_, W_)
    x = _L0_conv_ref(x, L0_conv_gn_w, L0_conv_gn_b, L0_conv_qkv_w, L0_conv_qkv_b, L0_conv_proj_w, L0_conv_proj_b)
    x = _L1_conv_ref(x, L1_conv_Wq, L1_conv_bq, L1_conv_Wk, L1_conv_bk, L1_conv_Wv, L1_conv_bv, L1_conv_gamma)
    return x

_drawn_inputs = setup_inputs


def setup_inputs(seed=0):
    import zlib

    import numpy as np

    out = dict(_drawn_inputs(seed))
    spreads = {'L0_conv_gn_w': (1.0, 0.2), 'L0_conv_gn_b': (0.0, 0.1)}
    factors = {'L0_conv_proj_b': 2.794,
     'L1_conv_Wq': 8.0,
     'L1_conv_bq': 8.0,
     'L1_conv_Wk': 8.0,
     'L1_conv_bk': 8.0,
     'L1_conv_Wv': 8.0,
     'L1_conv_bv': 8.0}
    for name, (base, spread) in spreads.items():
        noise = np.random.default_rng([zlib.crc32(name.encode()), seed]).standard_normal(out[name].shape)
        drawn = base * np.exp(spread * noise) if base else spread * noise
        out[name] = jnp.asarray(drawn.astype(out[name].dtype))
    for name, factor in factors.items():
        out[name] = (out[name] * factor).astype(out[name].dtype)
    return out
```

```python
from contextlib import ExitStack

import concourse.bass as bass
from concourse import mybir

F32 = mybir.dt.float32
F16 = mybir.dt.float16
ALU = mybir.AluOpType
ACT = mybir.ActivationFunctionType
AX = mybir.AxisListType

IMAGES = 32
C = 128
N = 1024
HALF = 512
TILES = N // C
PER_HALF = TILES // 2
CQK = C // 8
GROUP = C // 32
EPS = 1e-5
W_UP = 64.0
P_UP = 4096.0
STACK = 96
BN = 6


class Image:

    def __init__(self, pair, parity):
        self.pair, self.p = pair, parity
        self.n = pair * 2 + parity

    def before(self, d):
        q = self.p - d
        return Image(self.pair + q // 2, q % 2)

    def exists(self):
        return not isinstance(self.n, int) or 0 <= self.n < IMAGES


def every_iteration(engine, body):
    for it in range(3):
        body(Image(it // 2, it % 2))
    with engine.Fori(1, IMAGES // 2 - 1) as pair:
        body(Image(pair, 1))
        body(Image(pair + 1, 0))
    for it in range(IMAGES - 1, IMAGES + 3):
        body(Image(it // 2, it % 2))


def build(nc, x, gn_w, gn_b, qkv_w, qkv_b, proj_w, proj_b, Wq, bq, Wk, bk, Wv, bv, gamma, out):
    ctx = ExitStack()
    with ctx:
        def sb(name, shape, dt=F32):
            return ctx.enter_context(nc.sbuf_tensor(name, shape, dt))

        def sem(name):
            return ctx.enter_context(nc.semaphore(name))

        x_img = x.rearrange("b c h w -> b c (h w)")
        out_img = out.rearrange("b c h w -> b c (h w)")

        ident = sb("ident", [C, C])
        group_mean = sb("group_mean", [C, C])
        w_qkv = sb("w_qkv", [C, 3, C])
        w_proj = sb("w_proj", [C, C])
        w_vproj_t = sb("w_proj_t", [C, C])
        w_head = sb("w_head", [C, 3, C], F16)
        w_tail = sb("w_tail", [C, 3, C], F16)
        w1_qk = sb("w1_qk", [2 * CQK, C])
        w1_qk_t = sb("w1_qk_t", [C, 2, C])
        w1_v = sb("w1_v", [C, C])
        w1_v_t = sb("w1_v_t", [C, C])
        gnw = sb("gnw", [C, 1])
        gnb = sb("gnb", [C, 1])
        b_q = sb("b_q", [C, 1])
        b_k = sb("b_k", [C, 1])
        b_v = sb("b_v", [C, 1])
        b_proj = sb("b_proj", [C, 1])
        bias0 = sb("bias0", [C, 1])
        b1_q = sb("b1_q", [C, 1])
        b1_k = sb("b1_k", [C, 1])
        b1_v = sb("b1_v", [C, 1])
        gam = sb("gam", [C, 1])
        gam_down = sb("gam_down", [C, 1])
        gam_bv = sb("gam_bv", [C, 1])
        xb = sb("xb", [C, 2, N])
        stats = sb("stats", [C, 2, BN])
        mv = sb("mv", [C, 2])
        minus_half = sb("minus_half", [C, 1])
        gs = sb("gs", [C, 8])
        h32 = sb("h32", [C, N])
        h_head = sb("h_head", [C, N], F16)
        h_tail = sb("h_tail", [C, N], F16)
        qk32 = sb("qk32", [C, 2, 2, HALF])
        qk_head = sb("qk_head", [C, 2, 2, N], F16)
        qk_tail = sb("qk_tail", [C, 2, 2, N], F16)
        v_head = sb("v_head", [C, TILES, C], F16)
        v_tail = sb("v_tail", [C, TILES, C], F16)
        x1 = sb("x1", [C, 2, N])
        qk1_32 = sb("qk1_32", [C, 2, 2, HALF])
        qk1 = sb("qk1", [C, 2, 2, N], F16)
        v1_head = sb("v1_head", [C, TILES, C], F16)
        v1_tail = sb("v1_tail", [C, TILES, C], F16)
        y = sb("y", [C, 2, HALF])
        prob = [sb(f"prob{l}", [C, 2, N]) for l in range(2)]
        nmax = [sb(f"nmax{l}", [C, TILES]) for l in range(2)]
        rsum = [sb(f"rsum{l}", [C, TILES]) for l in range(2)]
        rinv = [sb(f"rinv{l}", [C, TILES]) for l in range(2)]
        pt_head = [sb(f"pt_head{l}", [C, 2, TILES, HALF], F16) for l in range(2)]
        pt_tail = [sb(f"pt_tail{l}", [C, 2, TILES, HALF], F16) for l in range(2)]

        scores = [ctx.enter_context(nc.psum_tensor(f"scores{l}", [C, N], F32)) for l in range(2)]
        turned = [ctx.enter_context(nc.psum_tensor(f"turned{l}", [C, HALF], F32)) for l in range(2)]
        side = [ctx.enter_context(nc.psum_tensor(f"side{l}", [C, HALF], F32)) for l in range(2)]

        setup_loaded = sem("setup_loaded")
        waited = sem("waited")
        waited_dve = sem("waited_dve")
        zeroed = sem("zeroed")
        consts_made = sem("consts_made")
        setup_pe = sem("setup_pe")
        setup_dve = sem("setup_dve")
        x_loaded = [sem(f"x_loaded{p}") for p in range(2)]
        y_stored = [sem(f"y_stored{h}") for h in range(2)]
        gn_dve = sem("gn_dve")
        gn_pe = sem("gn_pe")
        gn_root = sem("gn_root")
        h32_done = sem("h32_done")
        h_head_done = sem("h_head_done")
        h_tail_done = sem("h_tail_done")
        x_biased = sem("x_biased")
        qk_made = sem("qk_made")
        qk_out = sem("qk_out")
        qk_headed = sem("qk_headed")
        qk_tailed = sem("qk_tailed")
        v_made = sem("v_made")
        v_headed = sem("v_headed")
        v_tailed = sem("v_tailed")
        qk1_made = sem("qk1_made")
        qk1_out = sem("qk1_out")
        qk1_headed = sem("qk1_headed")
        qk1_tailed = sem("qk1_tailed")
        v1_made = sem("v1_made")
        v1_headed = sem("v1_headed")
        v1_tailed = sem("v1_tailed")
        x1_done = sem("x1_done")
        x1_biased = sem("x1_biased")
        y_done = sem("y_done")
        scored = [sem(f"scored{l}") for l in range(2)]
        maxed = [sem(f"maxed{l}") for l in range(2)]
        exped = [sem(f"exped{l}") for l in range(2)]
        inverted = [sem(f"inverted{l}") for l in range(2)]
        normed = [sem(f"normed{l}") for l in range(2)]
        transposed = [sem(f"transposed{l}") for l in range(2)]
        pt_headed = [sem(f"pt_headed{l}") for l in range(2)]
        pt_tailed = [sem(f"pt_tailed{l}") for l in range(2)]
        attended = [sem(f"attended{l}") for l in range(2)]

        block = ctx.enter_context(nc.Block())
        GN_STEPS = 9
        SETUP_DVE_ALL = 14
        QK_BANK = (1, 1, 0, 0)
        N_LOADS = 21
        K_SIDE, Q_SIDE = 1, 0

        def tile_of(layer, it, k):
            if layer == 0:
                return it, k
            return (it.before(2), k + 4) if k < 4 else (it.before(1), k - 4)

        def previous_tile(layer, it, k):
            return tile_of(layer, it.before(1), 7) if k == 0 else tile_of(layer, it, k - 1)

        def skip(im):
            return not im.exists()

        @block.sync
        def _(sp):
            col = lambda v: v.rearrange("(p a) -> p a", a=1)
            loads = [(w_qkv[:, j, :], qkv_w[j * C:(j + 1) * C, :]) for j in range(3)]
            loads += [(w_proj[:, :], proj_w), (w1_v[:, :], Wv), (w1_qk[0:CQK, :], Wq),
                      (w1_qk[CQK:2 * CQK, :], Wk), (gnw[:, :], col(gn_w)), (gnb[:, :], col(gn_b)),
                      (b_q[:, :], col(qkv_b[0:C])), (b_k[:, :], col(qkv_b[C:2 * C])),
                      (b_v[:, :], col(qkv_b[2 * C:3 * C])), (b_proj[:, :], col(proj_b)),
                      (b1_v[:, :], col(bv)), (gam[:, :], col(gamma).partition_broadcast(C))]
            sp.dma_start(xb[:, 0, :], x_img[0]).then_inc(x_loaded[0], 16)
            sp.dma_start(xb[:, 1, :], x_img[1]).then_inc(x_loaded[1], 16)
            for dst, src in loads:
                sp.dma_start(dst, src).then_inc(setup_loaded, 16)
            sp.wait_ge(zeroed, 2)
            for r in range(0, STACK, 32):
                sp.dma_start(b1_q[r:r + CQK, :], col(bq)).then_inc(setup_loaded, 16)
                sp.dma_start(b1_k[r:r + CQK, :], col(bk)).then_inc(setup_loaded, 16)

            def body(it):
                gone, nxt, y_im = it.before(1), it.before(-1), it.before(2)
                im = it.before(3)
                if not skip(im):
                    sp.wait_ge(y_done, im.n * 2 + 2)
                    sp.dma_start(out_img[im.n, :, HALF:N], y[:, 1, :]).then_inc(y_stored[1], 16)
                if not skip(gone) and not skip(nxt):
                    sp.wait_ge(x1_done, gone.n * 2 + 2)
                    sp.dma_start(xb[:, nxt.p, :], x_img[nxt.n]).then_inc(x_loaded[nxt.p], 16)
                if not skip(y_im):
                    sp.wait_ge(y_done, y_im.n * 2 + 1)
                    sp.dma_start(out_img[y_im.n, :, 0:HALF], y[:, 0, :]).then_inc(y_stored[0], 16)

            every_iteration(sp, body)
            for h in range(2):
                sp.wait_ge(y_stored[h], 16 * IMAGES)

        @block.gpsimd
        def _(pool):
            nc.gpsimd.memset(b1_q[:, :], 0.0).then_inc(zeroed, 1)
            nc.gpsimd.memset(b1_k[:, :], 0.0).then_inc(zeroed, 1)
            nc.gpsimd.memset(w1_qk_t[:, :, :], 0.0).then_inc(consts_made, 1)
            nc.gpsimd.memset(ident[:, :], 0.0).then_inc(consts_made, 1)
            nc.gpsimd.memset(group_mean[:, :], 1.0 / GROUP).then_inc(consts_made, 1)
            pool.wait_ge(consts_made, 3)
            nc.gpsimd.affine_select(out=ident[:, :], in_=ident[:, :], compare_op=ALU.not_equal, fill=1.0,
                                    base=0, pattern=[[-1, C]], channel_multiplier=1).then_inc(consts_made, 1)
            gm = group_mean[:, :].rearrange("p (g e) -> p g e", e=GROUP)
            nc.gpsimd.affine_select(out=gm, in_=gm, compare_op=ALU.is_ge, fill=0.0, base=0,
                                    pattern=[[-GROUP, C // GROUP], [0, GROUP]],
                                    channel_multiplier=1).then_inc(consts_made, 1)
            nc.gpsimd.memset(minus_half[:, :], -0.5).then_inc(consts_made, 1)
            pool.wait_ge(consts_made, 6)
            nc.gpsimd.affine_select(out=gm, in_=gm, compare_op=ALU.is_ge, fill=0.0, base=GROUP - 1,
                                    pattern=[[GROUP, C // GROUP], [0, GROUP]],
                                    channel_multiplier=-1).then_inc(consts_made, 1)

            def stand_apart():
                pool.sem_inc(waited, 1)

            def normalise(layer, it, k):
                im, t = tile_of(layer, it, k)
                if skip(im):
                    return
                pool.wait_ge(inverted[layer], im.n * TILES + t + 1)
                stand_apart()
                nc.gpsimd.tensor_scalar(prob[layer][:, t % 2, :], prob[layer][:, t % 2, :],
                                        rinv[layer][:, t:t + 1], P_UP, ALU.mult,
                                        ALU.mult).then_inc(normed[layer], 1)

            def gn_rsqrt(im):
                pool.wait_ge(gn_dve, im.n * GN_STEPS + 7)
                nc.gpsimd.tensor_tensor(gs[:, 3:4], gs[:, 6:7], minus_half[:, :],
                                        ALU.pow).then_inc(gn_root, 1)

            def h_split(im):
                pool.wait_ge(gn_dve, im.n * GN_STEPS + GN_STEPS)
                if not (isinstance(im.n, int) and im.n == 0):
                    pool.wait_ge(v_made, im.n * 2)
                stand_apart()
                nc.gpsimd.tensor_scalar(h32[:, :], xb[:, im.p, :], gs[:, 4:5], gs[:, 5:6], ALU.mult,
                                        ALU.subtract).then_inc(h32_done, 1)
                pool.wait_ge(h_head_done, im.n + 1)
                pool.wait_ge(h32_done, im.n + 1)
                nc.gpsimd.tensor_tensor(h_tail[:, :], h32[:, :], h_head[:, :],
                                        ALU.subtract).then_inc(h_tail_done, 1)

            def x_bias(im):
                pool.wait_ge(h32_done, im.n + 1)
                pool.wait_ge(h_head_done, im.n + 1)
                stand_apart()
                if isinstance(im.n, int) and im.n == 0:
                    pool.wait_ge(setup_dve, SETUP_DVE_ALL)
                nc.gpsimd.tensor_scalar(xb[:, im.p, :], xb[:, im.p, :], bias0[:, 0:1], 1.0, ALU.add,
                                        ALU.mult).then_inc(x_biased, 1)

            def qk_split_tail(im, j):
                s, h = (K_SIDE, K_SIDE, Q_SIDE, Q_SIDE)[j], j % 2
                pool.wait_ge(qk_headed, im.n * 4 + j + 1)
                nc.gpsimd.tensor_tensor(qk_tail[:, im.p, s, h * HALF:(h + 1) * HALF], qk32[:, s, h, :],
                                        qk_head[:, im.p, s, h * HALF:(h + 1) * HALF],
                                        ALU.subtract).then_inc(qk_tailed, 1)

            def body(it):
                nxt, l0, l1 = it.before(-1), it.before(1), it.before(2)
                for k in range(8):
                    normalise(0, it, k)
                    normalise(1, it, k)
                    if k == 3 and not skip(l1):
                        pool.wait_ge(v1_made, l1.n * 2 + 2)
                        stand_apart()
                        nc.gpsimd.tensor_scalar(x1[:, l1.p, :], x1[:, l1.p, :], gam_bv[:, 0:1], 1.0,
                                                ALU.add, ALU.mult).then_inc(x1_biased, 1)
                    if not skip(nxt):
                        if k == 5:
                            gn_rsqrt(nxt)
                            h_split(nxt)
                        if k == 7:
                            for j in range(4):
                                qk_split_tail(nxt, j)
                            x_bias(nxt)

            first = Image(0, 0)
            gn_rsqrt(first)
            h_split(first)
            for j in range(4):
                qk_split_tail(first, j)
            x_bias(first)
            every_iteration(pool, body)

        @block.scalar
        def _(act):
            def exponent(layer, it, k):
                im, t = tile_of(layer, it, k)
                if skip(im):
                    return
                act.wait_ge(maxed[layer], im.n * TILES + t + 1)
                if not (isinstance(im.n, int) and im.n * TILES + t < 2):
                    act.wait_ge(transposed[layer], (im.n * TILES + t - 1) * 2)
                nc.scalar.activation(prob[layer][:, t % 2, :], scores[layer][:, :], ACT.Exp,
                                     bias=nmax[layer][:, t:t + 1], scale=1.0,
                                     accum_out=rsum[layer][:, t:t + 1]).then_inc(exped[layer], 1)

            def pt_head_out(layer, it, k, h):
                im, t = previous_tile(layer, it, k)
                if skip(im):
                    return
                act.wait_ge(transposed[layer], im.n * 16 + t * 2 + h + 1)
                at = (t % PER_HALF) * C
                nc.scalar.activation(
                    pt_head[layer][:, t // PER_HALF, PER_HALF * h:PER_HALF * (h + 1), at:at + C],
                    turned[layer][:, :].rearrange("p (j n) -> p j n", n=C), ACT.Copy
                ).then_inc(pt_headed[layer], 1)

            def qk_copy_out(im, j):
                s, h = (K_SIDE, K_SIDE, Q_SIDE, Q_SIDE)[j], j % 2
                act.wait_ge(qk_made, im.n * 4 + j + 1)
                if not (isinstance(im.n, int) and im.n == 0):
                    act.wait_ge(qk_tailed, im.n * 4 + j - 3)
                elif j == 0:
                    act.wait_ge(setup_dve, SETUP_DVE_ALL)
                src = side[QK_BANK[j]][:, :]
                if s == Q_SIDE:
                    nc.scalar.activation(qk32[:, s, h, :], src, ACT.Identity, bias=b_q[:, 0:1],
                                         scale=C ** -0.5 / W_UP).then_inc(qk_out, 1)
                else:
                    nc.scalar.activation(qk32[:, s, h, :], src, ACT.Identity, bias=b_k[:, 0:1],
                                         scale=1.0 / W_UP).then_inc(qk_out, 1)

            def qk1_copy_out(im, j):
                s, h = (K_SIDE, Q_SIDE)[j % 2], j // 2
                act.wait_ge(qk1_made, im.n * 4 + j + 1)
                if not (isinstance(im.n, int) and im.n == 0):
                    act.wait_ge(qk1_tailed, im.n * 4 + j - 3)
                bias = b1_k if s == K_SIDE else b1_q
                nc.scalar.activation(qk1_32[:, s, h, :], side[0][:, :], ACT.Identity,
                                     bias=bias[:, 0:1], scale=1.0).then_inc(qk1_out, 1)

            def v_head_out(im, h):
                act.wait_ge(v_made, im.n * 2 + h + 1)
                nc.scalar.activation(v_head[:, PER_HALF * h:PER_HALF * (h + 1), :],
                                     side[0][:, :].rearrange("p (t c) -> p t c", c=C), ACT.Copy,
                                     scale=1.0 / W_UP).then_inc(v_headed, 1)

            def v1_head_out(im, h):
                act.wait_ge(v1_made, im.n * 2 + h + 1)
                nc.scalar.activation(v1_head[:, PER_HALF * h:PER_HALF * (h + 1), :],
                                     side[1][:, :].rearrange("p (t c) -> p t c", c=C),
                                     ACT.Copy).then_inc(v1_headed, 1)

            def body(it):
                nxt, l0, l1 = it.before(-1), it.before(1), it.before(2)
                for k in range(8):
                    pt_head_out(0, it, k, 0)
                    exponent(0, it, k)
                    pt_head_out(1, it, k, 0)
                    if k == 0 and not skip(l0):
                        qk1_copy_out(l0, 0)
                    if k == 3 and not skip(l0):
                        qk1_copy_out(l0, 2)
                    if k == 4 and not skip(it):
                        v_head_out(it, 0)
                    if k == 6 and not skip(nxt):
                        qk_copy_out(nxt, 0)
                    if k == 7 and not skip(nxt):
                        qk_copy_out(nxt, 2)
                    if k in (1, 2) and not skip(l1):
                        v1_head_out(l1, k - 1)
                    exponent(1, it, k)
                    pt_head_out(0, it, k, 1)
                    pt_head_out(1, it, k, 1)
                    if k == 0 and not skip(l0):
                        qk1_copy_out(l0, 1)
                    if k == 3 and not skip(l0):
                        qk1_copy_out(l0, 3)
                    if k == 4 and not skip(it):
                        v_head_out(it, 1)
                    if k == 6 and not skip(nxt):
                        qk_copy_out(nxt, 1)
                    if k == 7 and not skip(nxt):
                        qk_copy_out(nxt, 3)

            for j in range(4):
                qk_copy_out(Image(0, 0), j)
            act.wait_ge(setup_loaded, 16 * N_LOADS)
            every_iteration(act, body)

        @block.vector
        def _(dve):
            def row_max(layer, it, k):
                im, t = tile_of(layer, it, k)
                if skip(im):
                    return
                dve.wait_ge(scored[layer], im.n * TILES + t + 1)
                nc.vector.reduce_max(nmax[layer][:, t:t + 1], scores[layer][:, :], AX.X,
                                     negate=True).then_inc(maxed[layer], 1)

            def invert(layer, it, k):
                im, t = tile_of(layer, it, k)
                if skip(im):
                    return
                dve.wait_ge(exped[layer], im.n * TILES + t + 1)
                nc.vector.reciprocal(rinv[layer][:, t:t + 1],
                                     rsum[layer][:, t:t + 1]).then_inc(inverted[layer], 1)

            def pt_tail_out(layer, it, k, h):
                im, t = previous_tile(layer, it, k)
                if skip(im):
                    return
                dve.wait_ge(pt_headed[layer], im.n * 16 + t * 2 + h + 1)
                at = (t % PER_HALF) * C
                part = (slice(None), t // PER_HALF, slice(PER_HALF * h, PER_HALF * (h + 1)),
                        slice(at, at + C))
                nc.vector.tensor_tensor(pt_tail[layer][part],
                                        turned[layer][:, :].rearrange("p (j n) -> p j n", n=C),
                                        pt_head[layer][part], ALU.subtract).then_inc(pt_tailed[layer], 1)

            def gn_first(im):
                s = im.n * GN_STEPS
                dve.wait_ge(x_loaded[im.p], im.pair * 16 + 16)
                if not (isinstance(im.n, int) and im.n == 0):
                    dve.wait_ge(h32_done, im.n)
                for h in range(2):
                    nc.vector.bn_stats(stats[:, h, :], xb[:, im.p, h * HALF:(h + 1) * HALF]).then_inc(gn_dve, 1)
                dve.wait_ge(gn_dve, s + 2)
                dve.sem_inc(waited_dve, 1)
                nc.vector.bn_aggr(mv[:, :], stats[:, :, :]).then_inc(gn_dve, 1)

            def gn_second(im):
                s = im.n * GN_STEPS
                dve.wait_ge(gn_dve, s + 3)
                dve.wait_ge(gn_pe, im.n * 2 + 1)
                nc.vector.tensor_copy(gs[:, 0:1], side[1][:, 0:1]).then_inc(gn_dve, 1)
                dve.wait_ge(gn_dve, s + 4)
                nc.vector.tensor_tensor(gs[:, 1:2], mv[:, 0:1], gs[:, 0:1], ALU.subtract).then_inc(gn_dve, 1)
                dve.wait_ge(gn_dve, s + 5)
                nc.vector.tensor_scalar(gs[:, 2:3], gs[:, 1:2], gs[:, 1:2], mv[:, 1:2], ALU.mult,
                                        ALU.add).then_inc(gn_dve, 1)

            def gn_third(im):
                s = im.n * GN_STEPS
                dve.wait_ge(gn_pe, im.n * 2 + 2)
                nc.vector.tensor_scalar(gs[:, 6:7], side[1][:, 1:2], EPS, 1.0, ALU.add,
                                        ALU.mult).then_inc(gn_dve, 1)
                dve.wait_ge(gn_root, im.n + 1)
                nc.vector.tensor_tensor(gs[:, 4:5], gs[:, 3:4], gnw[:, :], ALU.mult).then_inc(gn_dve, 1)
                dve.wait_ge(gn_dve, s + 8)
                nc.vector.tensor_scalar(gs[:, 5:6], gs[:, 0:1], gs[:, 4:5], gnb[:, 0:1], ALU.mult,
                                        ALU.subtract).then_inc(gn_dve, 1)
                dve.wait_ge(gn_dve, s + 9)
                if not (isinstance(im.n, int) and im.n == 0):
                    dve.wait_ge(v_made, im.n * 2)
                nc.vector.tensor_scalar(h_head[:, :], xb[:, im.p, :], gs[:, 4:5], gs[:, 5:6], ALU.mult,
                                        ALU.subtract).then_inc(h_head_done, 1)

            def qk_head_copy(im, j):
                s, h = (K_SIDE, K_SIDE, Q_SIDE, Q_SIDE)[j], j % 2
                dve.wait_ge(qk_out, im.n * 4 + j + 1)
                nc.vector.tensor_copy(qk_head[:, im.p, s, h * HALF:(h + 1) * HALF],
                                      qk32[:, s, h, :]).then_inc(qk_headed, 1)

            def qk1_split(im, j):
                s, h = (K_SIDE, Q_SIDE)[j % 2], j // 2
                r = 32 if s == K_SIDE else 64
                cols = slice(h * HALF, (h + 1) * HALF)
                dve.wait_ge(qk1_out, im.n * 4 + j + 1)
                nc.vector.tensor_copy(qk1[0:STACK, im.p, s, cols],
                                      qk1_32[0:STACK, s, h, :]).then_inc(qk1_headed, 1)
                dve.wait_ge(qk1_headed, im.n * 4 + j + 1)
                nc.vector.tensor_tensor(qk1[r:r + 32, im.p, s, cols], qk1_32[r:r + 32, s, h, :],
                                        qk1[r:r + 32, im.p, s, cols], ALU.subtract).then_inc(qk1_tailed, 1)

            def v_tail_out(im, h):
                dve.wait_ge(v_headed, im.n * 2 + h + 1)
                part = (slice(None), slice(PER_HALF * h, PER_HALF * (h + 1)), slice(None))
                nc.vector.scalar_tensor_tensor(out=v_tail[part],
                                               in0=side[0][:, :].rearrange("p (t c) -> p t c", c=C),
                                               scalar=1.0 / W_UP, in1=v_head[part], op0=ALU.mult,
                                               op1=ALU.subtract).then_inc(v_tailed, 1)

            def v1_tail_out(im, h):
                dve.wait_ge(v1_headed, im.n * 2 + h + 1)
                part = (slice(None), slice(PER_HALF * h, PER_HALF * (h + 1)), slice(None))
                nc.vector.tensor_tensor(v1_tail[part], side[1][:, :].rearrange("p (t c) -> p t c", c=C),
                                        v1_head[part], ALU.subtract).then_inc(v1_tailed, 1)

            def x1_out(im, h):
                cols = slice(h * HALF, (h + 1) * HALF)
                dve.wait_ge(attended[0], im.n * 2 + h + 1)
                dve.wait_ge(x_biased, im.n + 1)
                if not (isinstance(im.n, int) and im.n < 2):
                    dve.wait_ge(y_done, (im.n - 2) * 2 + h + 1)
                nc.vector.scalar_tensor_tensor(out=x1[:, im.p, cols], in0=side[0][:, :], scalar=1.0 / P_UP,
                                               in1=xb[:, im.p, cols], op0=ALU.mult,
                                               op1=ALU.add).then_inc(x1_done, 1)

            def y_out(im, h):
                cols = slice(h * HALF, (h + 1) * HALF)
                dve.wait_ge(attended[1], im.n * 2 + h + 1)
                dve.wait_ge(x1_biased, im.n + 1)
                if not (isinstance(im.n, int) and im.n == 0):
                    dve.wait_ge(y_stored[h], im.n * 16)
                nc.vector.scalar_tensor_tensor(out=y[:, h, :], in0=side[1][:, :], scalar=gam_down[:, 0:1],
                                               in1=x1[:, im.p, cols], op0=ALU.mult,
                                               op1=ALU.add).then_inc(y_done, 1)

            dve.wait_ge(setup_loaded, 16 * N_LOADS)
            gn_first(Image(0, 0))
            gn_second(Image(0, 0))
            gn_third(Image(0, 0))
            for j in range(2):
                dve.wait_ge(setup_pe, j + 1)
                nc.vector.tensor_scalar(w_head[:, j, :], scores[0][:, j * C:(j + 1) * C], W_UP, 1.0,
                                        ALU.mult, ALU.mult).then_inc(setup_dve, 1)
                dve.wait_ge(setup_dve, 2 * j + 1)
                nc.vector.scalar_tensor_tensor(out=w_tail[:, j, :], in0=scores[0][:, j * C:(j + 1) * C],
                                               scalar=W_UP, in1=w_head[:, j, :], op0=ALU.mult,
                                               op1=ALU.subtract).then_inc(setup_dve, 1)
            dve.wait_ge(setup_pe, 3)
            nc.vector.tensor_copy(w_vproj_t[:, :], scores[0][:, 2 * C:3 * C]).then_inc(setup_dve, 1)
            dve.wait_ge(setup_pe, 4)
            nc.vector.tensor_copy(w1_v_t[:, :], scores[0][:, 3 * C:4 * C]).then_inc(setup_dve, 1)
            dve.wait_ge(setup_pe, 5)
            dve.wait_ge(consts_made, 1)
            for s in range(2):
                src = scores[1][:, s * CQK:(s + 1) * CQK].rearrange("p (a c) -> p a c", a=1)
                dst = w1_qk_t[:, s, 0:STACK].rearrange("p (a c) -> p a c", c=32)[:, :, 0:CQK]
                nc.vector.tensor_copy(dst, src.to_broadcast([C, 3, CQK])).then_inc(setup_dve, 1)
            dve.wait_ge(setup_pe, 6)
            nc.vector.tensor_scalar(w_head[:, 2, :], scores[1][:, 2 * C:3 * C], W_UP, 1.0,
                                    ALU.mult, ALU.mult).then_inc(setup_dve, 1)
            dve.wait_ge(setup_dve, 9)
            nc.vector.scalar_tensor_tensor(out=w_tail[:, 2, :], in0=scores[1][:, 2 * C:3 * C],
                                           scalar=W_UP, in1=w_head[:, 2, :], op0=ALU.mult,
                                           op1=ALU.subtract).then_inc(setup_dve, 1)
            dve.wait_ge(setup_pe, 7)
            nc.vector.tensor_tensor(bias0[:, :], scores[1][:, C:C + 1], b_proj[:, :], ALU.add).then_inc(setup_dve, 1)
            nc.vector.tensor_scalar(gam_down[:, :], gam[:, :], 1.0 / P_UP, 1.0, ALU.mult, ALU.mult).then_inc(setup_dve, 1)
            nc.vector.tensor_tensor(gam_bv[:, :], gam[:, :], b1_v[:, :], ALU.mult).then_inc(setup_dve, 1)
            nc.vector.tensor_scalar(b_q[:, :], b_q[:, :], C ** -0.5, 1.0, ALU.mult, ALU.mult).then_inc(setup_dve, 1)
            for j in range(4):
                qk_head_copy(Image(0, 0), j)

            def body(it):
                nxt, l0, l1 = it.before(-1), it.before(1), it.before(2)
                for k in range(8):
                    row_max(0, it, k)
                    pt_tail_out(0, it, k, 0)
                    row_max(1, it, k)
                    if k == 0 and not skip(l0):
                        qk1_split(l0, 0)
                    if k == 3 and not skip(l0):
                        qk1_split(l0, 2)
                    if k == 4 and not skip(it):
                        v_tail_out(it, 0)
                    if k == 6 and not skip(nxt):
                        qk_head_copy(nxt, 0)
                    if k == 7 and not skip(nxt):
                        qk_head_copy(nxt, 2)
                    if k in (1, 2) and not skip(l1):
                        v1_tail_out(l1, k - 1)
                    invert(0, it, k)
                    pt_tail_out(1, it, k, 0)
                    pt_tail_out(0, it, k, 1)
                    invert(1, it, k)
                    pt_tail_out(1, it, k, 1)
                    if k == 0 and not skip(l0):
                        qk1_split(l0, 1)
                    if k == 3 and not skip(l0):
                        qk1_split(l0, 3)
                    if k == 4 and not skip(it):
                        v_tail_out(it, 1)
                    if k == 6 and not skip(nxt):
                        qk_head_copy(nxt, 1)
                    if k == 7 and not skip(nxt):
                        qk_head_copy(nxt, 3)
                    if k == 0 and not skip(it.before(3)):
                        y_out(it.before(3), 1)
                    if k == 2 and not skip(l0):
                        x1_out(l0, 1)
                    if k == 4:
                        if not skip(l1):
                            y_out(l1, 0)
                        if not skip(nxt):
                            gn_first(nxt)
                    if k == 5 and not skip(nxt):
                        gn_second(nxt)
                        gn_third(nxt)
                    if k == 6 and not skip(it):
                        x1_out(it, 0)

            every_iteration(dve, body)

        @block.tensor
        def _(pe):
            mm = nc.tensor.matmul

            def split_product(dst, a_head, a_tail, b_head, b_tail, start=True, stop=True):
                mm(dst, a_head, b_head, start=start, stop=False)
                mm(dst, a_head, b_tail, start=False, stop=False)
                return mm(dst, a_tail, b_head, start=False, stop=stop)

            def score(layer, it, k):
                im, t = tile_of(layer, it, k)
                if skip(im):
                    return
                first = isinstance(im.n, int) and im.n * TILES + t == 0
                if not first:
                    pe.wait_ge(exped[layer], im.n * TILES + t)
                rows = slice(t * C, (t + 1) * C)
                if layer == 0:
                    if t in (0, 4):
                        pe.wait_ge(qk_tailed, im.n * 4 + (3 if t == 0 else 4))
                    for h in range(2):
                        cols = slice(h * HALF, (h + 1) * HALF)
                        last = split_product(scores[0][:, cols],
                                             qk_head[:, im.p, Q_SIDE, rows], qk_tail[:, im.p, Q_SIDE, rows],
                                             qk_head[:, im.p, K_SIDE, cols], qk_tail[:, im.p, K_SIDE, cols])
                else:
                    if t in (0, 4):
                        pe.wait_ge(qk1_tailed, im.n * 4 + (3 if t == 0 else 4))
                    for h in range(2):
                        cols = slice(h * HALF, (h + 1) * HALF)
                        last = mm(scores[1][:, cols], qk1[0:STACK, im.p, Q_SIDE, rows],
                                  qk1[0:STACK, im.p, K_SIDE, cols], start=True, stop=True)
                last.then_inc(scored[layer], 1)

            def transpose_half(layer, it, k, h):
                im, t = previous_tile(layer, it, k)
                if skip(im):
                    return
                if h == 0:
                    pe.wait_ge(normed[layer], im.n * TILES + t + 1)
                if not (isinstance(im.n, int) and im.n * 16 + t * 2 + h == 0):
                    pe.wait_ge(pt_tailed[layer], im.n * 16 + t * 2 + h)
                for j in range(PER_HALF):
                    m = (PER_HALF * h + j) * C
                    last = nc.tensor.transpose(turned[layer][:, j * C:(j + 1) * C],
                                               prob[layer][:, t % 2, m:m + C], ident[:, :])
                last.then_inc(transposed[layer], 1)

            def attend(layer, im, h, quarter):
                if skip(im):
                    return
                if quarter == 0:
                    pe.wait_ge(pt_tailed[layer], im.n * 16 + 8 * (h + 1))
                    if layer == 0:
                        pe.wait_ge(v_tailed, im.n * 2 + 2)
                        if h == 1:
                            pe.wait_ge(qk1_out, im.n * 4 + 2)
                    else:
                        pe.wait_ge(v1_tailed, im.n * 2 + 2)
                        if h == 1 and not skip(im.before(-3)):
                            pe.wait_ge(qk_out, im.n * 4 + 14)
                        elif h == 1:
                            pe.wait_ge(y_done, im.n * 2 + 1)
                head, tail = (v_head, v_tail) if layer == 0 else (v1_head, v1_tail)
                for t in (2 * quarter, 2 * quarter + 1):
                    last = split_product(side[layer][:, :], head[:, t, :], tail[:, t, :],
                                         pt_head[layer][:, h, t, :], pt_tail[layer][:, h, t, :],
                                         start=(t == 0), stop=(t == TILES - 1))
                if quarter == 3:
                    last.then_inc(attended[layer], 1)

            def qk_project(im, j):
                s, h = (K_SIDE, K_SIDE, Q_SIDE, Q_SIDE)[j], j % 2
                first = isinstance(im.n, int) and im.n == 0
                if j == 0:
                    pe.wait_ge(h_tail_done, im.n + 1)
                    if first:
                        pe.wait_ge(setup_dve, 4)
                    else:
                        pe.wait_ge(h_head_done, im.n + 1)
                elif j == 2 and not first:
                    pe.wait_ge(x1_done, im.n * 2 - 1)
                else:
                    pe.wait_ge(qk_out, im.n * 4 + j)
                cols = slice(h * HALF, (h + 1) * HALF)
                split_product(side[QK_BANK[j]][:, :], w_head[:, s, :], w_tail[:, s, :], h_head[:, cols],
                              h_tail[:, cols]).then_inc(qk_made, 1)

            def v_project(im, h):
                if h == 0:
                    if not skip(im.before(1)):
                        pe.wait_ge(qk1_out, im.n * 4)
                    elif isinstance(im.n, int):
                        pe.wait_ge(setup_dve, SETUP_DVE_ALL)
                        pe.wait_ge(qk_out, 4)
                else:
                    pe.wait_ge(v_tailed, im.n * 2 + 1)
                for j in range(PER_HALF):
                    rows = slice((PER_HALF * h + j) * C, (PER_HALF * h + j + 1) * C)
                    last = split_product(side[0][:, j * C:(j + 1) * C], h_head[:, rows], h_tail[:, rows],
                                         w_head[:, 2, :], w_tail[:, 2, :])
                last.then_inc(v_made, 1)

            def qk1_project(im, j):
                s, h = (K_SIDE, Q_SIDE)[j % 2], j // 2
                pe.wait_ge(x1_done, im.n * 2 + h + 1)
                if j == 0:
                    if not skip(im.before(-1)):
                        pe.wait_ge(qk_out, im.n * 4 + 8)
                elif j != 2:
                    pe.wait_ge(qk1_out, im.n * 4 + j)
                cols = slice(h * HALF, (h + 1) * HALF)
                mm(side[0][:, :], w1_qk_t[:, s, :], x1[:, im.p, cols], start=True,
                   stop=True).then_inc(qk1_made, 1)

            def v1_project(im, h):
                if h == 0:
                    if not skip(im.before(1)):
                        pe.wait_ge(y_done, im.n * 2)
                else:
                    pe.wait_ge(v1_tailed, im.n * 2 + 1)
                for j in range(PER_HALF):
                    rows = slice((PER_HALF * h + j) * C, (PER_HALF * h + j + 1) * C)
                    last = mm(side[1][:, j * C:(j + 1) * C], x1[:, im.p, rows], w1_v_t[:, :],
                              start=True, stop=True)
                last.then_inc(v1_made, 1)

            def gn_product(im, step):
                if step == 0:
                    if not skip(im.before(3)):
                        pe.wait_ge(y_done, im.n * 2 - 5)
                    pe.wait_ge(gn_dve, im.n * GN_STEPS + 3)
                    src = mv[:, 0:1]
                else:
                    pe.wait_ge(gn_dve, im.n * GN_STEPS + 6)
                    src = gs[:, 2:3]
                mm(side[1][:, step:step + 1], group_mean[:, :], src, start=True,
                   stop=True).then_inc(gn_pe, 1)

            pe.wait_ge(consts_made, 7)
            pe.wait_ge(setup_loaded, 16 * N_LOADS)
            gn_product(Image(0, 0), 0)
            for j in range(2):
                nc.tensor.transpose(scores[0][:, j * C:(j + 1) * C], w_qkv[:, j, :], ident[:, :]).then_inc(setup_pe, 1)
            nc.tensor.transpose(scores[0][:, 2 * C:3 * C], w_proj[:, :], ident[:, :]).then_inc(setup_pe, 1)
            nc.tensor.transpose(scores[0][:, 3 * C:4 * C], w1_v[:, :], ident[:, :]).then_inc(setup_pe, 1)
            nc.tensor.transpose(scores[1][:, 0:2 * CQK], w1_qk[:, :],
                                ident[0:2 * CQK, 0:2 * CQK]).then_inc(setup_pe, 1)
            gn_product(Image(0, 0), 1)
            pe.wait_ge(setup_dve, 8)
            mm(scores[1][:, 2 * C:3 * C], w_qkv[:, 2, :], w_vproj_t[:, :], start=True, stop=True).then_inc(setup_pe, 1)
            pe.wait_ge(setup_dve, 10)
            mm(scores[1][:, C:C + 1], w_vproj_t[:, :], b_v[:, :], start=True, stop=True).then_inc(setup_pe, 1)
            pe.wait_ge(setup_dve, SETUP_DVE_ALL)
            for j in range(4):
                qk_project(Image(0, 0), j)

            def body(it):
                nxt, l0, l1 = it.before(-1), it.before(1), it.before(2)
                attends = {0: (1, it.before(3), 1, 2), 1: (0, l0, 1, 0), 2: (0, l0, 1, 2),
                           3: (1, l1, 0, 0), 4: (1, l1, 0, 2), 5: (0, it, 0, 0), 6: (0, it, 0, 2),
                           7: (1, l1, 1, 0)}
                for k in range(8):
                    layer, im, h, quarter = attends[k]
                    score(0, it, k)
                    transpose_half(0, it, k, 0)
                    if k == 0 and not skip(l0):
                        qk1_project(l0, 0)
                    if k == 3 and not skip(l0):
                        qk1_project(l0, 2)
                    if k == 4 and not skip(it):
                        v_project(it, 0)
                    if k == 6 and not skip(nxt):
                        qk_project(nxt, 0)
                    if k == 7 and not skip(nxt):
                        qk_project(nxt, 2)
                    if k in (1, 2) and not skip(l1):
                        v1_project(l1, k - 1)
                    score(1, it, k)
                    transpose_half(1, it, k, 0)
                    attend(layer, im, h, quarter)
                    if k == 5 and not skip(nxt):
                        gn_product(nxt, 0)
                    transpose_half(0, it, k, 1)
                    transpose_half(1, it, k, 1)
                    if k == 5 and not skip(nxt):
                        gn_product(nxt, 1)
                    if k == 0 and not skip(l0):
                        qk1_project(l0, 1)
                    if k == 3 and not skip(l0):
                        qk1_project(l0, 3)
                    if k == 4 and not skip(it):
                        v_project(it, 1)
                    if k == 6 and not skip(nxt):
                        qk_project(nxt, 1)
                    if k == 7 and not skip(nxt):
                        qk_project(nxt, 3)
                    attend(layer, im, h, quarter + 1)

            every_iteration(pe, body)


_INS = ['x', 'L0_conv_gn_w', 'L0_conv_gn_b', 'L0_conv_qkv_w', 'L0_conv_qkv_b', 'L0_conv_proj_w',
        'L0_conv_proj_b', 'L1_conv_Wq', 'L1_conv_bq', 'L1_conv_Wk', 'L1_conv_bk', 'L1_conv_Wv',
        'L1_conv_bv', 'L1_conv_gamma']


def kernel(**inputs):
    import numpy as _np
    import concourse.bacc as _bacc
    from concourse import mybir as _mybir
    from concourse.bass_utils import run_bass_kernel_spmd as _run

    nc = _bacc.Bacc("TRN2", target_bir_lowering=False, num_devices=1)
    arrays, args = {}, []
    for name in _INS:
        a = _np.ascontiguousarray(inputs[name])
        arrays[f"in_{name}_dram"] = a
        args.append(nc.dram_tensor(f"in_{name}_dram", a.shape, _mybir.dt.from_np(a.dtype), kind="ExternalInput").ap())
    out = nc.dram_tensor("out_dram", inputs['x'].shape, _mybir.dt.float32, kind="ExternalOutput").ap()
    build(nc, *args, out)
    r = _run(nc, [arrays], core_ids=[0])
    return r.results[0]["out_dram"]
```

```python
from contextlib import ExitStack

import concourse.bass as bass
from concourse import mybir

F32 = mybir.dt.float32
F16 = mybir.dt.float16
ALU = mybir.AluOpType
ACT = mybir.ActivationFunctionType
AX = mybir.AxisListType

IMAGES = 32
C = 128
N = 1024
HALF = 512
TILES = N // C
PER_HALF = TILES // 2
CQK = C // 8
GROUP = C // 32
EPS = 1e-5
W_UP = 64.0
P_UP = 4096.0
STACK = 96
BN = 6


class Image:

    def __init__(self, pair, parity):
        self.pair, self.p = pair, parity
        self.n = pair * 2 + parity

    def before(self, d):
        q = self.p - d
        return Image(self.pair + q // 2, q % 2)

    def exists(self):
        return not isinstance(self.n, int) or 0 <= self.n < IMAGES


def every_iteration(engine, body):
    for it in range(3):
        body(Image(it // 2, it % 2))
    with engine.Fori(1, IMAGES // 2 - 1) as pair:
        body(Image(pair, 1))
        body(Image(pair + 1, 0))
    for it in range(IMAGES - 1, IMAGES + 3):
        body(Image(it // 2, it % 2))


def build(nc, x, gn_w, gn_b, qkv_w, qkv_b, proj_w, proj_b, Wq, bq, Wk, bk, Wv, bv, gamma, out):
    ctx = ExitStack()
    with ctx:
        def sb(name, shape, dt=F32):
            return ctx.enter_context(nc.sbuf_tensor(name, shape, dt))

        def sem(name):
            return ctx.enter_context(nc.semaphore(name))

        x_img = x.rearrange("b c h w -> b c (h w)")
        out_img = out.rearrange("b c h w -> b c (h w)")

        ident = sb("ident", [C, C])
        group_mean = sb("group_mean", [C, C])
        w_qkv = sb("w_qkv", [C, 3, C])
        w_proj = sb("w_proj", [C, C])
        w_vproj_t = sb("w_proj_t", [C, C])
        w_head = sb("w_head", [C, 3, C], F16)
        w_tail = sb("w_tail", [C, 3, C], F16)
        w1_qk = sb("w1_qk", [2 * CQK, C])
        w1_qk_t = sb("w1_qk_t", [C, 2, C])
        w1_v = sb("w1_v", [C, C])
        w1_v_t = sb("w1_v_t", [C, C])
        gnw = sb("gnw", [C, 1])
        gnb = sb("gnb", [C, 1])
        b_q = sb("b_q", [C, 1])
        b_k = sb("b_k", [C, 1])
        b_v = sb("b_v", [C, 1])
        b_proj = sb("b_proj", [C, 1])
        bias0 = sb("bias0", [C, 1])
        b1_q = sb("b1_q", [C, 1])
        b1_k = sb("b1_k", [C, 1])
        b1_v = sb("b1_v", [C, 1])
        gam = sb("gam", [C, 1])
        gam_down = sb("gam_down", [C, 1])
        gam_bv = sb("gam_bv", [C, 1])
        x_raw = sb("x_raw", [C, N])
        xb = sb("xb", [C, 2, N])
        stats = sb("stats", [C, 2, BN])
        mv = sb("mv", [C, 2])
        minus_half = sb("minus_half", [C, 1])
        gs = sb("gs", [C, 8])
        h32 = sb("h32", [C, N])
        h_head = sb("h_head", [C, 2, N], F16)
        h_tail = sb("h_tail", [C, 2, N], F16)
        qk32 = sb("qk32", [C, 2, 2, HALF])
        qk_head = sb("qk_head", [C, 2, 2, N], F16)
        qk_tail = sb("qk_tail", [C, 2, 2, N], F16)
        v_head = sb("v_head", [C, TILES, C], F16)
        v_tail = sb("v_tail", [C, TILES, C], F16)
        x1 = sb("x1", [C, 2, N])
        qk1_32 = sb("qk1_32", [C, 2, 2, HALF])
        qk1 = sb("qk1", [C, 2, 2, N], F16)
        v1_head = sb("v1_head", [C, TILES, C], F16)
        v1_tail = sb("v1_tail", [C, TILES, C], F16)
        y = sb("y", [C, 2, HALF])
        prob = [sb(f"prob{l}", [C, 2, N]) for l in range(2)]
        nmax = [sb(f"nmax{l}", [C, TILES]) for l in range(2)]
        rsum = [sb(f"rsum{l}", [C, TILES]) for l in range(2)]
        rinv = [sb(f"rinv{l}", [C, TILES]) for l in range(2)]
        pt_head = [sb(f"pt_head{l}", [C, 2, TILES, HALF], F16) for l in range(2)]
        pt_tail = [sb(f"pt_tail{l}", [C, 2, TILES, HALF], F16) for l in range(2)]

        scores = [ctx.enter_context(nc.psum_tensor(f"scores{l}", [C, N], F32)) for l in range(2)]
        turned = [ctx.enter_context(nc.psum_tensor(f"turned{l}", [C, HALF], F32)) for l in range(2)]
        side = [ctx.enter_context(nc.psum_tensor(f"side{l}", [C, HALF], F32)) for l in range(2)]

        setup_loaded = sem("setup_loaded")
        waited = sem("waited")
        waited_dve = sem("waited_dve")
        zeroed = sem("zeroed")
        consts_made = sem("consts_made")
        setup_pe = sem("setup_pe")
        setup_dve = sem("setup_dve")
        x_loaded = [sem(f"x_loaded{p}") for p in range(2)]
        y_stored = [sem(f"y_stored{h}") for h in range(2)]
        gn_dve = sem("gn_dve")
        gn_pe = sem("gn_pe")
        gn_root = sem("gn_root")
        h32_done = sem("h32_done")
        h_head_done = sem("h_head_done")
        h_tail_done = sem("h_tail_done")
        x_biased = sem("x_biased")
        qk_made = sem("qk_made")
        qk_out = sem("qk_out")
        qk_headed = sem("qk_headed")
        qk_tailed = sem("qk_tailed")
        v_made = sem("v_made")
        v_headed = sem("v_headed")
        v_tailed = sem("v_tailed")
        qk1_made = sem("qk1_made")
        qk1_out = sem("qk1_out")
        qk1_headed = sem("qk1_headed")
        qk1_tailed = sem("qk1_tailed")
        v1_made = sem("v1_made")
        v1_headed = sem("v1_headed")
        v1_tailed = sem("v1_tailed")
        x1_done = sem("x1_done")
        x1_biased = sem("x1_biased")
        y_done = sem("y_done")
        scored = [sem(f"scored{l}") for l in range(2)]
        maxed = [sem(f"maxed{l}") for l in range(2)]
        exped = [sem(f"exped{l}") for l in range(2)]
        inverted = [sem(f"inverted{l}") for l in range(2)]
        normed = [sem(f"normed{l}") for l in range(2)]
        transposed = [sem(f"transposed{l}") for l in range(2)]
        pt_headed = [sem(f"pt_headed{l}") for l in range(2)]
        pt_tailed = [sem(f"pt_tailed{l}") for l in range(2)]
        attended = [sem(f"attended{l}") for l in range(2)]

        block = ctx.enter_context(nc.Block())
        GN_STEPS = 9
        SETUP_DVE_ALL = 14
        QK_BANK = (1, 1, 0, 0)
        N_LOADS = 21
        K_SIDE, Q_SIDE = 1, 0

        def tile_of(layer, it, k):
            if layer == 0:
                return it, k
            return (it.before(2), k + 4) if k < 4 else (it.before(1), k - 4)

        def previous_tile(layer, it, k):
            return tile_of(layer, it.before(1), 7) if k == 0 else tile_of(layer, it, k - 1)

        def skip(im):
            return not im.exists()

        @block.sync
        def _(sp):
            col = lambda v: v.rearrange("(p a) -> p a", a=1)
            loads = [(w_qkv[:, j, :], qkv_w[j * C:(j + 1) * C, :]) for j in range(3)]
            loads += [(w_proj[:, :], proj_w), (w1_v[:, :], Wv), (w1_qk[0:CQK, :], Wq),
                      (w1_qk[CQK:2 * CQK, :], Wk), (gnw[:, :], col(gn_w)), (gnb[:, :], col(gn_b)),
                      (b_q[:, :], col(qkv_b[0:C])), (b_k[:, :], col(qkv_b[C:2 * C])),
                      (b_v[:, :], col(qkv_b[2 * C:3 * C])), (b_proj[:, :], col(proj_b)),
                      (b1_v[:, :], col(bv)), (gam[:, :], col(gamma).partition_broadcast(C))]
            sp.dma_start(x_raw[:, :], x_img[0]).then_inc(x_loaded[0], 16)
            for dst, src in loads:
                sp.dma_start(dst, src).then_inc(setup_loaded, 16)
            sp.wait_ge(zeroed, 2)
            for r in range(0, STACK, 32):
                sp.dma_start(b1_q[r:r + CQK, :], col(bq)).then_inc(setup_loaded, 16)
                sp.dma_start(b1_k[r:r + CQK, :], col(bk)).then_inc(setup_loaded, 16)

            def load_x(im):
                sp.wait_ge(x_biased, im.n)
                sp.wait_ge(h_head_done, im.n)
                sp.dma_start(x_raw[:, :], x_img[im.n]).then_inc(x_loaded[im.p], 16)

            def body(it):
                nxt, second, first = it.before(-1), it.before(3), it.before(2)
                if not skip(nxt):
                    load_x(nxt)
                if not skip(second):
                    sp.wait_ge(y_done, second.n * 2 + 2)
                    sp.dma_start(out_img[second.n, :, HALF:N], y[:, 1, :]).then_inc(y_stored[1], 16)
                if not skip(first):
                    sp.wait_ge(y_done, first.n * 2 + 1)
                    sp.dma_start(out_img[first.n, :, 0:HALF], y[:, 0, :]).then_inc(y_stored[0], 16)

            every_iteration(sp, body)
            for h in range(2):
                sp.wait_ge(y_stored[h], 16 * IMAGES)

        @block.gpsimd
        def _(pool):
            nc.gpsimd.memset(b1_q[:, :], 0.0).then_inc(zeroed, 1)
            nc.gpsimd.memset(b1_k[:, :], 0.0).then_inc(zeroed, 1)
            nc.gpsimd.memset(w1_qk_t[:, :, :], 0.0).then_inc(consts_made, 1)
            nc.gpsimd.memset(ident[:, :], 0.0).then_inc(consts_made, 1)
            nc.gpsimd.memset(group_mean[:, :], 1.0 / GROUP).then_inc(consts_made, 1)
            pool.wait_ge(consts_made, 3)
            nc.gpsimd.affine_select(out=ident[:, :], in_=ident[:, :], compare_op=ALU.not_equal, fill=1.0,
                                    base=0, pattern=[[-1, C]], channel_multiplier=1).then_inc(consts_made, 1)
            gm = group_mean[:, :].rearrange("p (g e) -> p g e", e=GROUP)
            nc.gpsimd.affine_select(out=gm, in_=gm, compare_op=ALU.is_ge, fill=0.0, base=0,
                                    pattern=[[-GROUP, C // GROUP], [0, GROUP]],
                                    channel_multiplier=1).then_inc(consts_made, 1)
            nc.gpsimd.memset(minus_half[:, :], -0.5).then_inc(consts_made, 1)
            pool.wait_ge(consts_made, 6)
            nc.gpsimd.affine_select(out=gm, in_=gm, compare_op=ALU.is_ge, fill=0.0, base=GROUP - 1,
                                    pattern=[[GROUP, C // GROUP], [0, GROUP]],
                                    channel_multiplier=-1).then_inc(consts_made, 1)

            def stand_apart():
                pool.sem_inc(waited, 1)

            def normalise(layer, it, k):
                im, t = tile_of(layer, it, k)
                if skip(im):
                    return
                pool.wait_ge(inverted[layer], im.n * TILES + t + 1)
                stand_apart()
                nc.gpsimd.tensor_scalar(prob[layer][:, t % 2, :], prob[layer][:, t % 2, :],
                                        rinv[layer][:, t:t + 1], P_UP, ALU.mult,
                                        ALU.mult).then_inc(normed[layer], 1)

            def gn_rsqrt(im):
                pool.wait_ge(gn_dve, im.n * GN_STEPS + 7)
                nc.gpsimd.tensor_tensor(gs[:, 3:4], gs[:, 6:7], minus_half[:, :],
                                        ALU.pow).then_inc(gn_root, 1)

            def h_split(im):
                pool.wait_ge(gn_dve, im.n * GN_STEPS + GN_STEPS)
                if not (isinstance(im.n, int) and im.n == 0):
                    pool.wait_ge(h_tail_done, im.n)
                stand_apart()
                nc.gpsimd.tensor_scalar(h32[:, :], x_raw[:, :], gs[:, 4:5], gs[:, 5:6], ALU.mult,
                                        ALU.subtract).then_inc(h32_done, 1)
                pool.wait_ge(h_head_done, im.n + 1)
                pool.wait_ge(h32_done, im.n + 1)
                nc.gpsimd.tensor_tensor(h_tail[:, im.p, :], h32[:, :], h_head[:, im.p, :],
                                        ALU.subtract).then_inc(h_tail_done, 1)

            def x_bias(im):
                if isinstance(im.n, int) and im.n == 0:
                    pool.wait_ge(setup_dve, SETUP_DVE_ALL)
                if not (isinstance(im.n, int) and im.n < 2):
                    pool.wait_ge(x1_done, im.n * 2 - 2)
                    stand_apart()
                nc.gpsimd.tensor_scalar(xb[:, im.p, :], x_raw[:, :], bias0[:, 0:1], 1.0, ALU.add,
                                        ALU.mult).then_inc(x_biased, 1)

            def qk_split_tail(im, j):
                s, h = (K_SIDE, K_SIDE, Q_SIDE, Q_SIDE)[j], j % 2
                pool.wait_ge(qk_headed, im.n * 4 + j + 1)
                nc.gpsimd.tensor_tensor(qk_tail[:, im.p, s, h * HALF:(h + 1) * HALF], qk32[:, s, h, :],
                                        qk_head[:, im.p, s, h * HALF:(h + 1) * HALF],
                                        ALU.subtract).then_inc(qk_tailed, 1)

            def body(it):
                nxt, l1 = it.before(-1), it.before(2)
                for k in range(8):
                    if k == 7 and not skip(nxt):
                        qk_split_tail(nxt, 1)
                    normalise(0, it, k)
                    if k in (6, 7) and not skip(nxt):
                        qk_split_tail(nxt, 2 * (k - 6))
                    normalise(1, it, k)
                    if k == 2 and not skip(l1):
                        pool.wait_ge(v1_made, l1.n * 2 + 2)
                        stand_apart()
                        nc.gpsimd.tensor_scalar(x1[:, l1.p, :], x1[:, l1.p, :], gam_bv[:, 0:1], 1.0,
                                                ALU.add, ALU.mult).then_inc(x1_biased, 1)
                    if not skip(nxt):
                        if k == 2:
                            gn_rsqrt(nxt)
                        if k == 3:
                            h_split(nxt)
                        if k == 4:
                            x_bias(nxt)
                        if k == 7:
                            qk_split_tail(nxt, 3)

            first = Image(0, 0)
            gn_rsqrt(first)
            h_split(first)
            for j in range(4):
                qk_split_tail(first, j)
            x_bias(first)
            every_iteration(pool, body)

        @block.scalar
        def _(act):
            def exponent(layer, it, k):
                im, t = tile_of(layer, it, k)
                if skip(im):
                    return
                act.wait_ge(maxed[layer], im.n * TILES + t + 1)
                if not (isinstance(im.n, int) and im.n * TILES + t < 2):
                    act.wait_ge(transposed[layer], (im.n * TILES + t - 1) * 2)
                nc.scalar.activation(prob[layer][:, t % 2, :], scores[layer][:, :], ACT.Exp,
                                     bias=nmax[layer][:, t:t + 1], scale=1.0,
                                     accum_out=rsum[layer][:, t:t + 1]).then_inc(exped[layer], 1)

            def pt_head_out(layer, it, k, h):
                im, t = previous_tile(layer, it, k)
                if skip(im):
                    return
                act.wait_ge(transposed[layer], im.n * 16 + t * 2 + h + 1)
                at = (t % PER_HALF) * C
                nc.scalar.activation(
                    pt_head[layer][:, t // PER_HALF, PER_HALF * h:PER_HALF * (h + 1), at:at + C],
                    turned[layer][:, :].rearrange("p (j n) -> p j n", n=C), ACT.Copy
                ).then_inc(pt_headed[layer], 1)

            def qk_copy_out(im, j):
                s, h = (K_SIDE, K_SIDE, Q_SIDE, Q_SIDE)[j], j % 2
                act.wait_ge(qk_made, im.n * 4 + j + 1)
                if not (isinstance(im.n, int) and im.n == 0):
                    act.wait_ge(qk_tailed, im.n * 4 + j - 3)
                elif j == 0:
                    act.wait_ge(setup_dve, SETUP_DVE_ALL)
                src = side[QK_BANK[j]][:, :]
                if s == Q_SIDE:
                    nc.scalar.activation(qk32[:, s, h, :], src, ACT.Identity, bias=b_q[:, 0:1],
                                         scale=C ** -0.5 / W_UP).then_inc(qk_out, 1)
                else:
                    nc.scalar.activation(qk32[:, s, h, :], src, ACT.Identity, bias=b_k[:, 0:1],
                                         scale=1.0 / W_UP).then_inc(qk_out, 1)

            def qk1_copy_out(im, j):
                s, h = (K_SIDE, Q_SIDE)[j % 2], j // 2
                act.wait_ge(qk1_made, im.n * 4 + j + 1)
                if not (isinstance(im.n, int) and im.n == 0):
                    act.wait_ge(qk1_tailed, im.n * 4 + j - 3)
                bias = b1_k if s == K_SIDE else b1_q
                nc.scalar.activation(qk1_32[:, s, h, :], side[0][:, :], ACT.Identity,
                                     bias=bias[:, 0:1], scale=1.0).then_inc(qk1_out, 1)

            def v_head_out(im, h):
                act.wait_ge(v_made, im.n * 2 + h + 1)
                nc.scalar.activation(v_head[:, PER_HALF * h:PER_HALF * (h + 1), :],
                                     side[0][:, :].rearrange("p (t c) -> p t c", c=C), ACT.Copy,
                                     scale=1.0 / W_UP).then_inc(v_headed, 1)

            def v1_head_out(im, h):
                act.wait_ge(v1_made, im.n * 2 + h + 1)
                nc.scalar.activation(v1_head[:, PER_HALF * h:PER_HALF * (h + 1), :],
                                     side[1][:, :].rearrange("p (t c) -> p t c", c=C),
                                     ACT.Copy).then_inc(v1_headed, 1)

            def extra(it, k, place):
                nxt, l0, l1 = it.before(-1), it.before(1), it.before(2)
                if k in (0, 3) and not skip(l0):
                    qk1_copy_out(l0, (0 if k == 0 else 2) + place)
                if k == 1 and not skip(l1):
                    v1_head_out(l1, place)
                if k == 4 and not skip(it):
                    v_head_out(it, place)
                if k in (6, 7) and not skip(nxt):
                    qk_copy_out(nxt, 2 * (k - 6) + place)

            def body(it):
                for k in range(8):
                    pt_head_out(0, it, k, 0)
                    pt_head_out(1, it, k, 0)
                    exponent(0, it, k)
                    extra(it, k, 0)
                    pt_head_out(0, it, k, 1)
                    exponent(1, it, k)
                    pt_head_out(1, it, k, 1)
                    extra(it, k, 1)

            for j in range(4):
                qk_copy_out(Image(0, 0), j)
            act.wait_ge(setup_loaded, 16 * N_LOADS)
            every_iteration(act, body)

        @block.vector
        def _(dve):
            def row_max(layer, it, k):
                im, t = tile_of(layer, it, k)
                if skip(im):
                    return
                dve.wait_ge(scored[layer], im.n * TILES + t + 1)
                nc.vector.reduce_max(nmax[layer][:, t:t + 1], scores[layer][:, :], AX.X,
                                     negate=True).then_inc(maxed[layer], 1)

            def invert(layer, it, k):
                im, t = tile_of(layer, it, k)
                if skip(im):
                    return
                dve.wait_ge(exped[layer], im.n * TILES + t + 1)
                nc.vector.reciprocal(rinv[layer][:, t:t + 1],
                                     rsum[layer][:, t:t + 1]).then_inc(inverted[layer], 1)

            def pt_tail_out(layer, it, k, h):
                im, t = previous_tile(layer, it, k)
                if skip(im):
                    return
                dve.wait_ge(pt_headed[layer], im.n * 16 + t * 2 + h + 1)
                at = (t % PER_HALF) * C
                part = (slice(None), t // PER_HALF, slice(PER_HALF * h, PER_HALF * (h + 1)),
                        slice(at, at + C))
                nc.vector.tensor_tensor(pt_tail[layer][part],
                                        turned[layer][:, :].rearrange("p (j n) -> p j n", n=C),
                                        pt_head[layer][part], ALU.subtract).then_inc(pt_tailed[layer], 1)

            def gn_first(im):
                s = im.n * GN_STEPS
                dve.wait_ge(x_loaded[im.p], im.pair * 16 + 16)
                if not (isinstance(im.n, int) and im.n == 0):
                    dve.wait_ge(h32_done, im.n)
                for h in range(2):
                    nc.vector.bn_stats(stats[:, h, :], x_raw[:, h * HALF:(h + 1) * HALF]).then_inc(gn_dve, 1)
                dve.wait_ge(gn_dve, s + 2)
                dve.sem_inc(waited_dve, 1)
                nc.vector.bn_aggr(mv[:, :], stats[:, :, :]).then_inc(gn_dve, 1)

            def gn_second(im):
                s = im.n * GN_STEPS
                dve.wait_ge(gn_dve, s + 3)
                dve.wait_ge(gn_pe, im.n * 2 + 1)
                nc.vector.tensor_copy(gs[:, 0:1], side[1][:, 0:1]).then_inc(gn_dve, 1)
                dve.wait_ge(gn_dve, s + 4)
                nc.vector.tensor_tensor(gs[:, 1:2], mv[:, 0:1], gs[:, 0:1], ALU.subtract).then_inc(gn_dve, 1)
                dve.wait_ge(gn_dve, s + 5)
                nc.vector.tensor_scalar(gs[:, 2:3], gs[:, 1:2], gs[:, 1:2], mv[:, 1:2], ALU.mult,
                                        ALU.add).then_inc(gn_dve, 1)

            def gn_third(im):
                dve.wait_ge(gn_pe, im.n * 2 + 2)
                nc.vector.tensor_scalar(gs[:, 6:7], side[1][:, 1:2], EPS, 1.0, ALU.add,
                                        ALU.mult).then_inc(gn_dve, 1)

            def gn_fourth(im):
                s = im.n * GN_STEPS
                dve.wait_ge(gn_root, im.n + 1)
                nc.vector.tensor_tensor(gs[:, 4:5], gs[:, 3:4], gnw[:, :], ALU.mult).then_inc(gn_dve, 1)
                dve.wait_ge(gn_dve, s + 8)
                nc.vector.tensor_scalar(gs[:, 5:6], gs[:, 0:1], gs[:, 4:5], gnb[:, 0:1], ALU.mult,
                                        ALU.subtract).then_inc(gn_dve, 1)

            def h_head_out(im):
                dve.wait_ge(gn_dve, im.n * GN_STEPS + 9)
                if not (isinstance(im.n, int) and im.n < 2):
                    dve.wait_ge(v_made, im.n * 2 - 2)
                nc.vector.tensor_scalar(h_head[:, im.p, :], x_raw[:, :], gs[:, 4:5], gs[:, 5:6], ALU.mult,
                                        ALU.subtract).then_inc(h_head_done, 1)

            def qk_head_copy(im, j):
                s, h = (K_SIDE, K_SIDE, Q_SIDE, Q_SIDE)[j], j % 2
                dve.wait_ge(qk_out, im.n * 4 + j + 1)
                nc.vector.tensor_copy(qk_head[:, im.p, s, h * HALF:(h + 1) * HALF],
                                      qk32[:, s, h, :]).then_inc(qk_headed, 1)

            def qk1_split(im, j):
                s, h = (K_SIDE, Q_SIDE)[j % 2], j // 2
                r = 32 if s == K_SIDE else 64
                cols = slice(h * HALF, (h + 1) * HALF)
                dve.wait_ge(qk1_out, im.n * 4 + j + 1)
                nc.vector.tensor_copy(qk1[0:STACK, im.p, s, cols],
                                      qk1_32[0:STACK, s, h, :]).then_inc(qk1_headed, 1)
                dve.wait_ge(qk1_headed, im.n * 4 + j + 1)
                nc.vector.tensor_tensor(qk1[r:r + 32, im.p, s, cols], qk1_32[r:r + 32, s, h, :],
                                        qk1[r:r + 32, im.p, s, cols], ALU.subtract).then_inc(qk1_tailed, 1)

            def v_tail_out(im, h):
                dve.wait_ge(v_headed, im.n * 2 + h + 1)
                part = (slice(None), slice(PER_HALF * h, PER_HALF * (h + 1)), slice(None))
                nc.vector.scalar_tensor_tensor(out=v_tail[part],
                                               in0=side[0][:, :].rearrange("p (t c) -> p t c", c=C),
                                               scalar=1.0 / W_UP, in1=v_head[part], op0=ALU.mult,
                                               op1=ALU.subtract).then_inc(v_tailed, 1)

            def v1_tail_out(im, h):
                dve.wait_ge(v1_headed, im.n * 2 + h + 1)
                part = (slice(None), slice(PER_HALF * h, PER_HALF * (h + 1)), slice(None))
                nc.vector.tensor_tensor(v1_tail[part], side[1][:, :].rearrange("p (t c) -> p t c", c=C),
                                        v1_head[part], ALU.subtract).then_inc(v1_tailed, 1)

            def x1_out(im, h):
                cols = slice(h * HALF, (h + 1) * HALF)
                dve.wait_ge(attended[0], im.n * 2 + h + 1)
                dve.wait_ge(x_biased, im.n + 1)
                if not (isinstance(im.n, int) and im.n < 2):
                    dve.wait_ge(y_done, (im.n - 2) * 2 + h + 1)
                nc.vector.scalar_tensor_tensor(out=x1[:, im.p, cols], in0=side[0][:, :], scalar=1.0 / P_UP,
                                               in1=xb[:, im.p, cols], op0=ALU.mult,
                                               op1=ALU.add).then_inc(x1_done, 1)

            def y_out(im, h):
                cols = slice(h * HALF, (h + 1) * HALF)
                dve.wait_ge(attended[1], im.n * 2 + h + 1)
                dve.wait_ge(x1_biased, im.n + 1)
                if not (isinstance(im.n, int) and im.n == 0):
                    dve.wait_ge(y_stored[h], im.n * 16)
                nc.vector.scalar_tensor_tensor(out=y[:, h, :], in0=side[1][:, :], scalar=gam_down[:, 0:1],
                                               in1=x1[:, im.p, cols], op0=ALU.mult,
                                               op1=ALU.add).then_inc(y_done, 1)

            dve.wait_ge(setup_loaded, 16 * N_LOADS)
            gn_first(Image(0, 0))
            gn_second(Image(0, 0))
            gn_third(Image(0, 0))
            gn_fourth(Image(0, 0))
            h_head_out(Image(0, 0))
            for j in range(2):
                dve.wait_ge(setup_pe, j + 1)
                nc.vector.tensor_scalar(w_head[:, j, :], scores[0][:, j * C:(j + 1) * C], W_UP, 1.0,
                                        ALU.mult, ALU.mult).then_inc(setup_dve, 1)
                dve.wait_ge(setup_dve, 2 * j + 1)
                nc.vector.scalar_tensor_tensor(out=w_tail[:, j, :], in0=scores[0][:, j * C:(j + 1) * C],
                                               scalar=W_UP, in1=w_head[:, j, :], op0=ALU.mult,
                                               op1=ALU.subtract).then_inc(setup_dve, 1)
            dve.wait_ge(setup_pe, 3)
            nc.vector.tensor_copy(w_vproj_t[:, :], scores[0][:, 2 * C:3 * C]).then_inc(setup_dve, 1)
            dve.wait_ge(setup_pe, 4)
            nc.vector.tensor_copy(w1_v_t[:, :], scores[0][:, 3 * C:4 * C]).then_inc(setup_dve, 1)
            dve.wait_ge(setup_pe, 5)
            dve.wait_ge(consts_made, 1)
            for s in range(2):
                src = scores[1][:, s * CQK:(s + 1) * CQK].rearrange("p (a c) -> p a c", a=1)
                dst = w1_qk_t[:, s, 0:STACK].rearrange("p (a c) -> p a c", c=32)[:, :, 0:CQK]
                nc.vector.tensor_copy(dst, src.to_broadcast([C, 3, CQK])).then_inc(setup_dve, 1)
            dve.wait_ge(setup_pe, 6)
            nc.vector.tensor_scalar(w_head[:, 2, :], scores[1][:, 2 * C:3 * C], W_UP, 1.0,
                                    ALU.mult, ALU.mult).then_inc(setup_dve, 1)
            dve.wait_ge(setup_dve, 9)
            nc.vector.scalar_tensor_tensor(out=w_tail[:, 2, :], in0=scores[1][:, 2 * C:3 * C],
                                           scalar=W_UP, in1=w_head[:, 2, :], op0=ALU.mult,
                                           op1=ALU.subtract).then_inc(setup_dve, 1)
            dve.wait_ge(setup_pe, 7)
            nc.vector.tensor_tensor(bias0[:, :], scores[1][:, C:C + 1], b_proj[:, :], ALU.add).then_inc(setup_dve, 1)
            nc.vector.tensor_scalar(gam_down[:, :], gam[:, :], 1.0 / P_UP, 1.0, ALU.mult, ALU.mult).then_inc(setup_dve, 1)
            nc.vector.tensor_tensor(gam_bv[:, :], gam[:, :], b1_v[:, :], ALU.mult).then_inc(setup_dve, 1)
            nc.vector.tensor_scalar(b_q[:, :], b_q[:, :], C ** -0.5, 1.0, ALU.mult, ALU.mult).then_inc(setup_dve, 1)
            for j in range(4):
                qk_head_copy(Image(0, 0), j)

            def extra(it, k, place):
                nxt, l0, l1 = it.before(-1), it.before(1), it.before(2)
                if k in (0, 3) and not skip(l0):
                    qk1_split(l0, (0 if k == 0 else 2) + place)
                if k == 1 and not skip(l1):
                    v1_tail_out(l1, place)
                if k == 4 and not skip(it):
                    v_tail_out(it, place)
                if k in (6, 7) and not skip(nxt):
                    qk_head_copy(nxt, 2 * (k - 6) + place)

            def body(it):
                nxt, l0, l1 = it.before(-1), it.before(1), it.before(2)
                for k in range(8):
                    row_max(0, it, k)
                    pt_tail_out(0, it, k, 0)
                    row_max(1, it, k)
                    pt_tail_out(1, it, k, 0)
                    if k == 2 and not skip(nxt):
                        gn_second(nxt)
                    invert(0, it, k)
                    extra(it, k, 0)
                    pt_tail_out(0, it, k, 1)
                    if k == 2 and not skip(nxt):
                        gn_third(nxt)
                    invert(1, it, k)
                    pt_tail_out(1, it, k, 1)
                    extra(it, k, 1)
                    if k == 0 and not skip(it.before(3)):
                        y_out(it.before(3), 1)
                    if k == 1 and not skip(nxt):
                        gn_first(nxt)
                    if k == 2 and not skip(nxt):
                        gn_fourth(nxt)
                    if k == 2 and not skip(l0):
                        x1_out(l0, 1)
                    if k == 3 and not skip(nxt):
                        h_head_out(nxt)
                    if k == 4 and not skip(l1):
                        y_out(l1, 0)
                    if k == 6 and not skip(it):
                        x1_out(it, 0)

            every_iteration(dve, body)

        @block.tensor
        def _(pe):
            mm = nc.tensor.matmul

            def split_product(dst, a_head, a_tail, b_head, b_tail, start=True, stop=True):
                mm(dst, a_head, b_head, start=start, stop=False)
                mm(dst, a_head, b_tail, start=False, stop=False)
                return mm(dst, a_tail, b_head, start=False, stop=stop)

            def score(layer, it, k):
                im, t = tile_of(layer, it, k)
                if skip(im):
                    return
                first = isinstance(im.n, int) and im.n * TILES + t == 0
                if not first:
                    pe.wait_ge(exped[layer], im.n * TILES + t)
                rows = slice(t * C, (t + 1) * C)
                if layer == 0:
                    if t in (0, 4):
                        pe.wait_ge(qk_tailed, im.n * 4 + (3 if t == 0 else 4))
                    for h in range(2):
                        cols = slice(h * HALF, (h + 1) * HALF)
                        last = split_product(scores[0][:, cols],
                                             qk_head[:, im.p, Q_SIDE, rows], qk_tail[:, im.p, Q_SIDE, rows],
                                             qk_head[:, im.p, K_SIDE, cols], qk_tail[:, im.p, K_SIDE, cols])
                else:
                    if t in (0, 4):
                        pe.wait_ge(qk1_tailed, im.n * 4 + (3 if t == 0 else 4))
                    for h in range(2):
                        cols = slice(h * HALF, (h + 1) * HALF)
                        last = mm(scores[1][:, cols], qk1[0:STACK, im.p, Q_SIDE, rows],
                                  qk1[0:STACK, im.p, K_SIDE, cols], start=True, stop=True)
                last.then_inc(scored[layer], 1)

            def transpose_half(layer, it, k, h):
                im, t = previous_tile(layer, it, k)
                if skip(im):
                    return
                if h == 0:
                    pe.wait_ge(normed[layer], im.n * TILES + t + 1)
                if not (isinstance(im.n, int) and im.n * 16 + t * 2 + h == 0):
                    pe.wait_ge(pt_tailed[layer], im.n * 16 + t * 2 + h)
                for j in range(PER_HALF):
                    m = (PER_HALF * h + j) * C
                    last = nc.tensor.transpose(turned[layer][:, j * C:(j + 1) * C],
                                               prob[layer][:, t % 2, m:m + C], ident[:, :])
                last.then_inc(transposed[layer], 1)

            def attend(layer, im, h, t):
                if skip(im):
                    return
                if t == 0:
                    pe.wait_ge(pt_tailed[layer], im.n * 16 + 8 * (h + 1))
                    if layer == 0:
                        pe.wait_ge(v_tailed, im.n * 2 + 2)
                        if h == 1:
                            pe.wait_ge(qk1_out, im.n * 4 + 2)
                    else:
                        pe.wait_ge(v1_tailed, im.n * 2 + 2)
                        ahead = im.before(-3)
                        if h == 0 and not skip(ahead):
                            pe.wait_ge(gn_dve, ahead.n * GN_STEPS + 7)
                        elif h == 1 and not skip(ahead):
                            pe.wait_ge(qk_out, ahead.n * 4 + 2)
                        elif h == 1:
                            pe.wait_ge(y_done, im.n * 2 + 1)
                head, tail = (v_head, v_tail) if layer == 0 else (v1_head, v1_tail)
                last = split_product(side[layer][:, :], head[:, t, :], tail[:, t, :],
                                     pt_head[layer][:, h, t, :], pt_tail[layer][:, h, t, :],
                                     start=(t == 0), stop=(t == TILES - 1))
                if t == TILES - 1:
                    last.then_inc(attended[layer], 1)

            def qk_project(im, j):
                s, h = (K_SIDE, K_SIDE, Q_SIDE, Q_SIDE)[j], j % 2
                first = isinstance(im.n, int) and im.n == 0
                if j == 0:
                    pe.wait_ge(h_tail_done, im.n + 1)
                    pe.wait_ge(h_head_done, im.n + 1)
                    if not skip(im.before(3)):
                        pe.wait_ge(y_done, im.n * 2 - 5)
                elif j == 2 and not first:
                    pe.wait_ge(x1_done, im.n * 2 - 1)
                else:
                    pe.wait_ge(qk_out, im.n * 4 + j)
                cols = slice(h * HALF, (h + 1) * HALF)
                split_product(side[QK_BANK[j]][:, :], w_head[:, s, :], w_tail[:, s, :],
                              h_head[:, im.p, cols], h_tail[:, im.p, cols]).then_inc(qk_made, 1)

            def v_project(im, h):
                if h == 0:
                    if not skip(im.before(1)):
                        pe.wait_ge(qk1_out, im.n * 4)
                    elif isinstance(im.n, int):
                        pe.wait_ge(setup_dve, SETUP_DVE_ALL)
                        pe.wait_ge(qk_out, 4)
                else:
                    pe.wait_ge(v_tailed, im.n * 2 + 1)
                for j in range(PER_HALF):
                    rows = slice((PER_HALF * h + j) * C, (PER_HALF * h + j + 1) * C)
                    last = split_product(side[0][:, j * C:(j + 1) * C], h_head[:, im.p, rows],
                                         h_tail[:, im.p, rows],
                                         w_head[:, 2, :], w_tail[:, 2, :])
                last.then_inc(v_made, 1)

            def qk1_project(im, j):
                s, h = (K_SIDE, Q_SIDE)[j % 2], j // 2
                pe.wait_ge(x1_done, im.n * 2 + h + 1)
                if j == 0:
                    if not skip(im.before(-1)):
                        pe.wait_ge(qk_out, im.n * 4 + 8)
                elif j != 2:
                    pe.wait_ge(qk1_out, im.n * 4 + j)
                cols = slice(h * HALF, (h + 1) * HALF)
                mm(side[0][:, :], w1_qk_t[:, s, :], x1[:, im.p, cols], start=True,
                   stop=True).then_inc(qk1_made, 1)

            def v1_project(im, h):
                if h == 0:
                    if not skip(im.before(1)):
                        pe.wait_ge(y_done, im.n * 2)
                else:
                    pe.wait_ge(v1_tailed, im.n * 2 + 1)
                for j in range(PER_HALF):
                    rows = slice((PER_HALF * h + j) * C, (PER_HALF * h + j + 1) * C)
                    last = mm(side[1][:, j * C:(j + 1) * C], x1[:, im.p, rows], w1_v_t[:, :],
                              start=True, stop=True)
                last.then_inc(v1_made, 1)

            def gn_product(im, step):
                if step == 0:
                    if not skip(im.before(3)):
                        pe.wait_ge(v1_tailed, im.n * 2 - 4)
                    pe.wait_ge(gn_dve, im.n * GN_STEPS + 3)
                    src = mv[:, 0:1]
                else:
                    pe.wait_ge(gn_dve, im.n * GN_STEPS + 6)
                    src = gs[:, 2:3]
                mm(side[1][:, step:step + 1], group_mean[:, :], src, start=True,
                   stop=True).then_inc(gn_pe, 1)

            pe.wait_ge(consts_made, 7)
            pe.wait_ge(setup_loaded, 16 * N_LOADS)
            gn_product(Image(0, 0), 0)
            for j in range(2):
                nc.tensor.transpose(scores[0][:, j * C:(j + 1) * C], w_qkv[:, j, :], ident[:, :]).then_inc(setup_pe, 1)
            nc.tensor.transpose(scores[0][:, 2 * C:3 * C], w_proj[:, :], ident[:, :]).then_inc(setup_pe, 1)
            nc.tensor.transpose(scores[0][:, 3 * C:4 * C], w1_v[:, :], ident[:, :]).then_inc(setup_pe, 1)
            nc.tensor.transpose(scores[1][:, 0:2 * CQK], w1_qk[:, :],
                                ident[0:2 * CQK, 0:2 * CQK]).then_inc(setup_pe, 1)
            gn_product(Image(0, 0), 1)
            pe.wait_ge(setup_dve, 8)
            mm(scores[1][:, 2 * C:3 * C], w_qkv[:, 2, :], w_vproj_t[:, :], start=True, stop=True).then_inc(setup_pe, 1)
            pe.wait_ge(setup_dve, 10)
            mm(scores[1][:, C:C + 1], w_vproj_t[:, :], b_v[:, :], start=True, stop=True).then_inc(setup_pe, 1)
            pe.wait_ge(setup_dve, SETUP_DVE_ALL)
            for j in range(4):
                qk_project(Image(0, 0), j)

            def extra(it, k, place):
                nxt, l0, l1 = it.before(-1), it.before(1), it.before(2)
                if k in (0, 3) and not skip(l0):
                    qk1_project(l0, (0 if k == 0 else 2) + place)
                if k == 1 and not skip(l1):
                    v1_project(l1, place)
                if k == 2 and not skip(nxt):
                    gn_product(nxt, place)
                if k == 4 and not skip(it):
                    v_project(it, place)
                if k in (6, 7) and not skip(nxt):
                    qk_project(nxt, 2 * (k - 6) + place)

            def body(it):
                l0, l1 = it.before(1), it.before(2)
                attends = {0: (1, it.before(3), 1, 4), 1: (0, l0, 1, 0), 2: (0, l0, 1, 4),
                           3: (1, l1, 0, 0), 4: (1, l1, 0, 4), 5: (0, it, 0, 0), 6: (0, it, 0, 4),
                           7: (1, l1, 1, 0)}
                for k in range(8):
                    layer, im, h, t = attends[k]
                    score(0, it, k)
                    transpose_half(0, it, k, 0)
                    attend(layer, im, h, t)
                    extra(it, k, 0)
                    score(1, it, k)
                    transpose_half(1, it, k, 0)
                    attend(layer, im, h, t + 1)
                    transpose_half(0, it, k, 1)
                    attend(layer, im, h, t + 2)
                    if k == 2:
                        extra(it, k, 1)
                    transpose_half(1, it, k, 1)
                    attend(layer, im, h, t + 3)
                    if k != 2:
                        extra(it, k, 1)

            every_iteration(pe, body)


_INS = ['x', 'L0_conv_gn_w', 'L0_conv_gn_b', 'L0_conv_qkv_w', 'L0_conv_qkv_b', 'L0_conv_proj_w',
        'L0_conv_proj_b', 'L1_conv_Wq', 'L1_conv_bq', 'L1_conv_Wk', 'L1_conv_bk', 'L1_conv_Wv',
        'L1_conv_bv', 'L1_conv_gamma']


def kernel(**inputs):
    import numpy as _np
    import concourse.bacc as _bacc
    from concourse import mybir as _mybir
    from concourse.bass_utils import run_bass_kernel_spmd as _run

    nc = _bacc.Bacc("TRN2", target_bir_lowering=False, num_devices=1)
    arrays, args = {}, []
    for name in _INS:
        a = _np.ascontiguousarray(inputs[name])
        arrays[f"in_{name}_dram"] = a
        args.append(nc.dram_tensor(f"in_{name}_dram", a.shape, _mybir.dt.from_np(a.dtype), kind="ExternalInput").ap())
    out = nc.dram_tensor("out_dram", inputs['x'].shape, _mybir.dt.float32, kind="ExternalOutput").ap()
    build(nc, *args, out)
    r = _run(nc, [arrays], core_ids=[0])
    return r.results[0]["out_dram"]
```

```python
from contextlib import ExitStack

import concourse.bass as bass
from concourse import mybir

F32 = mybir.dt.float32
F16 = mybir.dt.float16
ALU = mybir.AluOpType
ACT = mybir.ActivationFunctionType
AX = mybir.AxisListType

IMAGES = 32
C = 128
N = 1024
HALF = 512
TILES = N // C
PER_HALF = TILES // 2
CQK = C // 8
GROUP = C // 32
EPS = 1e-5
W_UP = 64.0
P_UP = 4096.0
STACK = 96
BN = 6


class Image:

    def __init__(self, pair, parity):
        self.pair, self.p = pair, parity
        self.n = pair * 2 + parity

    def before(self, d):
        q = self.p - d
        return Image(self.pair + q // 2, q % 2)

    def exists(self):
        return not isinstance(self.n, int) or 0 <= self.n < IMAGES


def every_iteration(engine, body):
    for it in range(3):
        body(Image(it // 2, it % 2))
    with engine.Fori(1, IMAGES // 2 - 2) as pair:
        body(Image(pair, 1))
        body(Image(pair + 1, 0))
    for it in range(IMAGES - 3, IMAGES + 1):
        body(Image(it // 2, it % 2))


def build(nc, x, gn_w, gn_b, qkv_w, qkv_b, proj_w, proj_b, Wq, bq, Wk, bk, Wv, bv, gamma, out):
    ctx = ExitStack()
    with ctx:
        def sb(name, shape, dt=F32):
            return ctx.enter_context(nc.sbuf_tensor(name, shape, dt))

        def sem(name):
            return ctx.enter_context(nc.semaphore(name))

        x_img = x.rearrange("b c h w -> b c (h w)")
        out_img = out.rearrange("b c h w -> b c (h w)")

        ident = sb("ident", [C, C])
        group_mean = sb("group_mean", [C, C])
        w_qkv = sb("w_qkv", [C, 3, C])
        w_proj = sb("w_proj", [C, C])
        w_vproj_t = sb("w_proj_t", [C, C])
        w_head = sb("w_head", [C, 3, C], F16)
        w_tail = sb("w_tail", [C, 3, C], F16)
        w1_qk = sb("w1_qk", [2 * CQK, C])
        w1_qk_t = sb("w1_qk_t", [C, STACK])
        w1_v = sb("w1_v", [C, C])
        w1_v_t = sb("w1_v_t", [C, C])
        gnw = sb("gnw", [C, 1])
        gnb = sb("gnb", [C, 1])
        b_q = sb("b_q", [C, 1])
        b_k = sb("b_k", [C, 1])
        b_v = sb("b_v", [C, 1])
        b_proj = sb("b_proj", [C, 1])
        bias0 = sb("bias0", [C, 1])
        b1_qk = sb("b1_qk", [C, 1])
        b1_v = sb("b1_v", [C, 1])
        gam = sb("gam", [C, 1])
        gam_down = sb("gam_down", [C, 1])
        gam_bv = sb("gam_bv", [C, 1])
        x_raw = sb("x_raw", [C, N])
        xb = sb("xb", [C, 2, N])
        stats = sb("stats", [C, 2, BN])
        mv = sb("mv", [C, 2])
        minus_half = sb("minus_half", [C, 1])
        gs = sb("gs", [C, 8])
        h32 = sb("h32", [C, N])
        h_head = sb("h_head", [C, 2, N], F16)
        h_tail = sb("h_tail", [C, 2, N], F16)
        qk32 = sb("qk32", [C, 2, 2, HALF])
        qk_head = sb("qk_head", [C, 2, 2, N], F16)
        qk_tail = sb("qk_tail", [C, 2, 2, N], F16)
        v_head = sb("v_head", [C, TILES, C], F16)
        v_tail = sb("v_tail", [C, TILES, C], F16)
        x1 = sb("x1", [C, 2, N])
        qk1 = sb("qk1", [C, 2, 2, N], F16)
        v1_head = sb("v1_head", [C, TILES, C], F16)
        v1_tail = sb("v1_tail", [C, TILES, C], F16)
        y = sb("y", [C, 2, HALF])
        prob = [sb(f"prob{l}", [C, 2, N]) for l in range(2)]
        nmax = [sb(f"nmax{l}", [C, TILES]) for l in range(2)]
        rsum = [sb(f"rsum{l}", [C, TILES]) for l in range(2)]
        rinv = [sb(f"rinv{l}", [C, TILES]) for l in range(2)]
        pt_head = [sb(f"pt_head{l}", [C, 2, TILES, HALF], F16) for l in range(2)]
        pt_tail = [sb(f"pt_tail{l}", [C, 2, TILES, HALF], F16) for l in range(2)]

        scores = [ctx.enter_context(nc.psum_tensor(f"scores{l}", [C, N], F32)) for l in range(2)]
        turned = [ctx.enter_context(nc.psum_tensor(f"turned{l}", [C, HALF], F32)) for l in range(2)]
        side = [ctx.enter_context(nc.psum_tensor(f"side{l}", [C, HALF], F32)) for l in range(2)]

        setup_loaded = sem("setup_loaded")
        gn_loaded = sem("gn_loaded")
        waited = sem("waited")
        waited_dve = sem("waited_dve")
        zeroed = sem("zeroed")
        consts_made = sem("consts_made")
        setup_pe = sem("setup_pe")
        setup_dve = sem("setup_dve")
        x_loaded = [sem(f"x_loaded{p}") for p in range(2)]
        y_stored = [sem(f"y_stored{h}") for h in range(2)]
        gn_dve = sem("gn_dve")
        gn_pe = sem("gn_pe")
        gn_root = sem("gn_root")
        h32_done = sem("h32_done")
        h_head_done = sem("h_head_done")
        h_tail_done = sem("h_tail_done")
        x_biased = sem("x_biased")
        qk_made = sem("qk_made")
        qk_out = sem("qk_out")
        qk_headed = sem("qk_headed")
        qk_tailed = sem("qk_tailed")
        v_made = sem("v_made")
        v_headed = sem("v_headed")
        v_tailed = sem("v_tailed")
        qk1_made = sem("qk1_made")
        qk1_headed = sem("qk1_headed")
        qk1_tailed = sem("qk1_tailed")
        v1_made = sem("v1_made")
        v1_headed = sem("v1_headed")
        v1_tailed = sem("v1_tailed")
        x1_done = sem("x1_done")
        x1_biased = sem("x1_biased")
        y_scaled = sem("y_scaled")
        y_done = sem("y_done")
        scored = [sem(f"scored{l}") for l in range(2)]
        maxed = [sem(f"maxed{l}") for l in range(2)]
        exped = [sem(f"exped{l}") for l in range(2)]
        inverted = [sem(f"inverted{l}") for l in range(2)]
        normed = [sem(f"normed{l}") for l in range(2)]
        transposed = [sem(f"transposed{l}") for l in range(2)]
        pt_headed = [sem(f"pt_headed{l}") for l in range(2)]
        pt_tailed = [sem(f"pt_tailed{l}") for l in range(2)]
        attended = [sem(f"attended{l}") for l in range(2)]

        block = ctx.enter_context(nc.Block())
        GN_STEPS = 10
        SETUP_DVE_ALL = 15
        V_PLACES = ((4, 0), (4, 1))
        QK_PLACES = ((5, 0), (5, 1), (6, 0), (7, 0))
        N_LOADS = 16
        K_SIDE, Q_SIDE = 1, 0

        def last(it):
            return isinstance(it.n, int) and it.n == IMAGES

        def tile_of(layer, it, k):
            if layer == 0:
                return (it, k - 4) if last(it) else (it, k)
            return (it.before(2), k + 4) if k < 4 else (it.before(1), k - 4)

        def previous_tile(layer, it, k):
            return tile_of(layer, it.before(1), 7) if k == 0 else tile_of(layer, it, k - 1)

        def qk_bank(im, j):
            return ((1, 0, 1, 0) if isinstance(im.n, int) and im.n == 0 else (1, 1, 1, 0))[j]

        def skip(im):
            return not im.exists()

        def no_tile(layer, im, t):
            return not 0 <= t < PER_HALF if layer == 0 and last(im) else skip(im)

        @block.sync
        def _(sp):
            col = lambda v: v.rearrange("(p a) -> p a", a=1)
            loads = [(w_qkv[:, j, :], qkv_w[j * C:(j + 1) * C, :]) for j in range(3)]
            loads += [(w_proj[:, :], proj_w), (w1_v[:, :], Wv), (w1_qk[0:CQK, :], Wq),
                      (w1_qk[CQK:2 * CQK, :], Wk)]
            sp.dma_start(x_raw[:, :], x_img[0]).then_inc(x_loaded[0], 16)
            for dst, src in loads:
                sp.dma_start(dst, src).then_inc(setup_loaded, 16)
            sp.wait_ge(zeroed, 1)
            for r, src in ((0, bq), (32, bq), (64, bk)):
                sp.dma_start(b1_qk[r:r + CQK, :], col(src)).then_inc(setup_loaded, 16)

            def load_x(im):
                sp.wait_ge(x_biased, im.n)
                sp.wait_ge(h32_done, im.n)
                sp.wait_ge(h_head_done, im.n)
                sp.dma_start(x_raw[:, :], x_img[im.n]).then_inc(x_loaded[im.p], 16)

            def body(it):
                ahead, second, first = it.before(-2), it.before(3), it.before(2)
                if not skip(second):
                    sp.wait_ge(y_done, second.n * 2 + 2)
                    sp.dma_start(out_img[second.n, :, HALF:N], y[:, 1, :]).then_inc(y_stored[1], 16)
                if not skip(ahead):
                    load_x(ahead)
                if not skip(first):
                    sp.wait_ge(y_done, first.n * 2 + 1)
                    sp.dma_start(out_img[first.n, :, 0:HALF], y[:, 0, :]).then_inc(y_stored[0], 16)

            load_x(Image(0, 1))
            every_iteration(sp, body)
            for n, h in ((IMAGES - 2, 1), (IMAGES - 1, 0), (IMAGES - 1, 1)):
                sp.wait_ge(y_done, n * 2 + h + 1)
                sp.dma_start(out_img[n, :, h * HALF:(h + 1) * HALF], y[:, h, :]).then_inc(y_stored[h], 16)
            for h in range(2):
                sp.wait_ge(y_stored[h], 16 * IMAGES)

        @block.gpsimd
        def _(pool):
            nc.gpsimd.memset(b1_qk[:, :], 0.0).then_inc(zeroed, 1)
            nc.gpsimd.memset(w1_qk_t[:, :], 0.0).then_inc(consts_made, 1)
            nc.gpsimd.memset(ident[:, :], 0.0).then_inc(consts_made, 1)
            nc.gpsimd.memset(group_mean[:, :], 1.0 / GROUP).then_inc(consts_made, 1)
            pool.wait_ge(consts_made, 3)
            nc.gpsimd.affine_select(out=ident[:, :], in_=ident[:, :], compare_op=ALU.not_equal, fill=1.0,
                                    base=0, pattern=[[-1, C]], channel_multiplier=1).then_inc(consts_made, 1)
            gm = group_mean[:, :].rearrange("p (g e) -> p g e", e=GROUP)
            nc.gpsimd.affine_select(out=gm, in_=gm, compare_op=ALU.is_ge, fill=0.0, base=0,
                                    pattern=[[-GROUP, C // GROUP], [0, GROUP]],
                                    channel_multiplier=1).then_inc(consts_made, 1)
            nc.gpsimd.memset(minus_half[:, :], -0.5).then_inc(consts_made, 1)
            pool.wait_ge(consts_made, 6)
            nc.gpsimd.affine_select(out=gm, in_=gm, compare_op=ALU.is_ge, fill=0.0, base=GROUP - 1,
                                    pattern=[[GROUP, C // GROUP], [0, GROUP]],
                                    channel_multiplier=-1).then_inc(consts_made, 1)

            def stand_apart():
                pool.sem_inc(waited, 1)

            def normalise(layer, it, k):
                im, t = tile_of(layer, it, k)
                if no_tile(layer, im, t):
                    return
                pool.wait_ge(inverted[layer], im.n * TILES + t + 1)
                stand_apart()
                nc.gpsimd.tensor_scalar(prob[layer][:, t % 2, :], prob[layer][:, t % 2, :],
                                        rinv[layer][:, t:t + 1], P_UP, ALU.mult,
                                        ALU.mult).then_inc(normed[layer], 1)

            def gn_rsqrt(im):
                pool.wait_ge(gn_dve, im.n * GN_STEPS + 7)
                nc.gpsimd.tensor_tensor(gs[:, 3:4], gs[:, 6:7], minus_half[:, :],
                                        ALU.pow).then_inc(gn_root, 1)

            def h_full(im):
                pool.wait_ge(gn_dve, im.n * GN_STEPS + GN_STEPS)
                if not (isinstance(im.n, int) and im.n == 0):
                    pool.wait_ge(h_tail_done, im.n)
                stand_apart()
                nc.gpsimd.tensor_scalar(h32[:, :], x_raw[:, :], gs[:, 4:5], gs[:, 5:6], ALU.mult,
                                        ALU.add).then_inc(h32_done, 1)

            def h_tail_out(im):
                pool.wait_ge(h_head_done, im.n + 1)
                pool.wait_ge(h32_done, im.n + 1)
                nc.gpsimd.tensor_tensor(h_tail[:, im.p, :], h32[:, :], h_head[:, im.p, :],
                                        ALU.subtract).then_inc(h_tail_done, 1)

            def y_out(im, h):
                cols = slice(h * HALF, (h + 1) * HALF)
                pool.wait_ge(y_scaled, im.n * 2 + h + 1)
                pool.wait_ge(x1_biased, im.n + 1)
                nc.gpsimd.tensor_tensor(y[:, h, :], y[:, h, :], x1[:, im.p, cols],
                                        ALU.add).then_inc(y_done, 1)

            def x1_bias(im):
                pool.wait_ge(v1_made, im.n * 2 + 2)
                stand_apart()
                nc.gpsimd.tensor_scalar(x1[:, im.p, :], x1[:, im.p, :], gam_bv[:, 0:1], 1.0,
                                        ALU.add, ALU.mult).then_inc(x1_biased, 1)

            def x_bias(im):
                pool.wait_ge(x_loaded[im.p], im.pair * 16 + 16)
                stand_apart()
                if isinstance(im.n, int) and im.n == 0:
                    pool.wait_ge(setup_dve, SETUP_DVE_ALL)
                if not (isinstance(im.n, int) and im.n < 2):
                    pool.wait_ge(x1_done, im.n * 2 - 2)
                    stand_apart()
                nc.gpsimd.tensor_scalar(xb[:, im.p, :], x_raw[:, :], bias0[:, 0:1], 1.0, ALU.add,
                                        ALU.mult).then_inc(x_biased, 1)

            def qk_split(im, j):
                s, h = (K_SIDE, K_SIDE, Q_SIDE, Q_SIDE)[j], j % 2
                pool.wait_ge(qk_out, im.n * 4 + j + 1)
                stand_apart()
                nc.gpsimd.tensor_scalar(qk_head[:, im.p, s, h * HALF:(h + 1) * HALF], qk32[:, s, h, :],
                                        1.0, 0.0, ALU.mult, ALU.add).then_inc(qk_headed, 1)
                if isinstance(im.n, int) and im.n == 0:
                    return
                pool.wait_ge(qk_headed, im.n * 4 + j + 1)
                nc.gpsimd.tensor_tensor(qk_tail[:, im.p, s, h * HALF:(h + 1) * HALF], qk32[:, s, h, :],
                                        qk_head[:, im.p, s, h * HALF:(h + 1) * HALF],
                                        ALU.subtract).then_inc(qk_tailed, 1)

            def body(it):
                nxt, l0, l1 = it.before(-1), it.before(1), it.before(2)
                for k in range(8):
                    if k == 4 and not skip(nxt):
                        h_tail_out(nxt)
                    if k == 6 and not skip(nxt):
                        qk_split(nxt, 1)
                    normalise(0, it, k)
                    normalise(1, it, k)
                    if k in (5, 6, 7) and not skip(nxt):
                        qk_split(nxt, (0, 2, 3)[k - 5])
                    if k == 0 and not skip(it.before(3)):
                        y_out(it.before(3), 1)
                    if k == 2 and not skip(l1):
                        x1_bias(l1)
                    if k == 7 and last(it):
                        y_out(l1, 1)
                    if k == 2 and not skip(nxt):
                        gn_rsqrt(nxt)
                    if k == 3 and not skip(nxt):
                        h_full(nxt)
                    if k == 4 and not skip(nxt):
                        x_bias(nxt)
                    if k == 4 and not skip(l1):
                        y_out(l1, 0)

            first = Image(0, 0)
            gn_rsqrt(first)
            h_full(first)
            h_tail_out(first)
            x_bias(first)
            for j in range(4):
                qk_split(first, j)
            every_iteration(pool, body)
            x1_bias(Image(IMAGES // 2 - 1, 1))
            for h in range(2):
                y_out(Image(IMAGES // 2 - 1, 1), h)

        @block.scalar
        def _(act):
            def exponent(layer, it, k):
                im, t = tile_of(layer, it, k)
                if no_tile(layer, im, t):
                    return
                act.wait_ge(maxed[layer], im.n * TILES + t + 1)
                if not (isinstance(im.n, int) and im.n * TILES + t < 2):
                    act.wait_ge(transposed[layer], (im.n * TILES + t - 1) * 2)
                nc.scalar.activation(prob[layer][:, t % 2, :], scores[layer][:, :], ACT.Exp,
                                     bias=nmax[layer][:, t:t + 1], scale=1.0,
                                     accum_out=rsum[layer][:, t:t + 1]).then_inc(exped[layer], 1)

            def pt_head_out(layer, it, k, h):
                im, t = previous_tile(layer, it, k)
                if no_tile(layer, im, t):
                    return
                act.wait_ge(transposed[layer], im.n * 16 + t * 2 + h + 1)
                at = (t % PER_HALF) * C
                nc.scalar.activation(
                    pt_head[layer][:, t // PER_HALF, PER_HALF * h:PER_HALF * (h + 1), at:at + C],
                    turned[layer][:, :].rearrange("p (j n) -> p j n", n=C), ACT.Copy
                ).then_inc(pt_headed[layer], 1)

            def qk_copy_out(im, j):
                s, h = (K_SIDE, K_SIDE, Q_SIDE, Q_SIDE)[j], j % 2
                act.wait_ge(qk_made, im.n * 4 + j + 1)
                if not (isinstance(im.n, int) and im.n == 0):
                    act.wait_ge(qk_tailed, im.n * 4 + j - 3)
                elif j == 0:
                    act.wait_ge(setup_dve, 5)
                src = side[qk_bank(im, j)][:, :]
                bias, scale = (b_q, C ** -0.5 / W_UP) if s == Q_SIDE else (b_k, 1.0 / W_UP)
                nc.scalar.activation(qk32[:, s, h, :], src, ACT.Identity, bias=bias[:, 0:1],
                                     scale=scale).then_inc(qk_out, 1)

            def qk1_head_out(im, h, keys):
                cols = slice(h * HALF, (h + 1) * HALF)
                act.wait_ge(qk1_made, im.n * 2 + h + 1)
                if not (isinstance(im.n, int) and im.n < 2):
                    act.wait_ge(scored[1], im.n * TILES - TILES)
                moves = (((64, 96), (64, 96)), ((0, 32), (64, 96))) if keys else (((0, 64), (0, 64)),)
                for into, out_of in moves:
                    nc.scalar.activation(qk1[into[0]:into[1], im.p, K_SIDE if keys else Q_SIDE, cols],
                                         side[0][out_of[0]:out_of[1], :], ACT.Identity,
                                         bias=b1_qk[out_of[0]:out_of[1], 0:1],
                                         scale=1.0).then_inc(qk1_headed, 1)

            def h_head_out(im):
                act.wait_ge(gn_dve, im.n * GN_STEPS + GN_STEPS)
                if not (isinstance(im.n, int) and im.n < 2):
                    act.wait_ge(v_made, im.n * 2 - 2)
                nc.scalar.activation(h_head[:, im.p, :], x_raw[:, :], ACT.Identity, bias=gs[:, 5:6],
                                     scale=gs[:, 4:5]).then_inc(h_head_done, 1)

            def y_scale(im, h):
                lane = 0 if isinstance(im.n, int) and im.n * 2 + h + 1 == IMAGES * 2 else 1
                act.wait_ge(attended[lane], im.n * 2 + h + (2 if lane == 0 else 1))
                if not (isinstance(im.n, int) and im.n == 0):
                    act.wait_ge(y_stored[h], im.n * 16)
                nc.scalar.activation(y[:, h, :], side[lane][:, :], ACT.Copy,
                                     scale=gam_down[:, 0:1]).then_inc(y_scaled, 1)

            def v_head_out(im, h):
                act.wait_ge(v_made, im.n * 2 + h + 1)
                nc.scalar.activation(v_head[:, PER_HALF * h:PER_HALF * (h + 1), :],
                                     side[0][:, :].rearrange("p (t c) -> p t c", c=C), ACT.Copy,
                                     scale=1.0 / W_UP).then_inc(v_headed, 1)

            def v1_head_out(im, h):
                act.wait_ge(v1_made, im.n * 2 + h + 1)
                nc.scalar.activation(v1_head[:, PER_HALF * h:PER_HALF * (h + 1), :],
                                     side[1][:, :].rearrange("p (t c) -> p t c", c=C),
                                     ACT.Copy).then_inc(v1_headed, 1)

            def extra(it, k, place):
                nxt, l0, l1 = it.before(-1), it.before(1), it.before(2)
                if k in (0, 3) and place == 0 and not skip(l0):
                    qk1_head_out(l0, k // 3, keys=False)
                    if k == 0:
                        qk1_head_out(l0, 0, keys=True)
                if k == 1 and not skip(l1):
                    v1_head_out(l1, place)
                if k == 7 and last(it):
                    v1_head_out(l0, place)
                if (k, place) in V_PLACES and not skip(it):
                    v_head_out(it, V_PLACES.index((k, place)))
                if (k, place) in QK_PLACES and not skip(nxt):
                    qk_copy_out(nxt, QK_PLACES.index((k, place)))

            def body(it):
                for k in range(8):
                    pt_head_out(0, it, k, 0)
                    extra(it, k, 0)
                    pt_head_out(1, it, k, 0)
                    exponent(0, it, k)
                    pt_head_out(0, it, k, 1)
                    if k == 3 and not skip(it.before(1)):
                        qk1_head_out(it.before(1), 1, keys=True)
                    exponent(1, it, k)
                    extra(it, k, 1)
                    pt_head_out(1, it, k, 1)
                    if k == 0 and not skip(it.before(3)):
                        y_scale(it.before(3), 1)
                    if k == 3 and not skip(it.before(-1)):
                        h_head_out(it.before(-1))
                    if k == 4 and not skip(it.before(2)):
                        y_scale(it.before(2), 0)
                    if k == 6 and last(it):
                        y_scale(it.before(2), 1)

            col = lambda v: v.rearrange("(p a) -> p a", a=1)
            act.dma_start(gnw[:, :], col(gn_w)).then_inc(gn_loaded, 16)
            act.dma_start(gnb[:, :], col(gn_b)).then_inc(gn_loaded, 16)
            for dst, src in ((b_q, col(qkv_b[0:C])), (b_k, col(qkv_b[C:2 * C])),
                             (b_v, col(qkv_b[2 * C:3 * C])), (b_proj, col(proj_b)), (b1_v, col(bv)),
                             (gam, col(gamma).partition_broadcast(C))):
                act.dma_start(dst[:, :], src).then_inc(setup_loaded, 16)
            h_head_out(Image(0, 0))
            for j in range(4):
                qk_copy_out(Image(0, 0), j)
            act.wait_ge(setup_loaded, 16 * N_LOADS)
            every_iteration(act, body)
            end = Image(IMAGES // 2, 1)
            for h in range(2):
                for lane in range(2):
                    pt_head_out(lane, end, 0, h)
            for h in range(2):
                y_scale(end.before(2), h)

        @block.vector
        def _(dve):
            def row_max(layer, it, k):
                im, t = tile_of(layer, it, k)
                if no_tile(layer, im, t):
                    return
                dve.wait_ge(scored[layer], im.n * TILES + t + 1)
                nc.vector.reduce_max(nmax[layer][:, t:t + 1], scores[layer][:, :], AX.X,
                                     negate=True).then_inc(maxed[layer], 1)

            def invert(layer, it, k):
                im, t = tile_of(layer, it, k)
                if no_tile(layer, im, t):
                    return
                dve.wait_ge(exped[layer], im.n * TILES + t + 1)
                nc.vector.reciprocal(rinv[layer][:, t:t + 1],
                                     rsum[layer][:, t:t + 1]).then_inc(inverted[layer], 1)

            def pt_tail_out(layer, it, k, h):
                im, t = previous_tile(layer, it, k)
                if no_tile(layer, im, t):
                    return
                dve.wait_ge(pt_headed[layer], im.n * 16 + t * 2 + h + 1)
                at = (t % PER_HALF) * C
                part = (slice(None), t // PER_HALF, slice(PER_HALF * h, PER_HALF * (h + 1)),
                        slice(at, at + C))
                nc.vector.tensor_tensor(pt_tail[layer][part],
                                        turned[layer][:, :].rearrange("p (j n) -> p j n", n=C),
                                        pt_head[layer][part], ALU.subtract).then_inc(pt_tailed[layer], 1)

            def gn_first(im, h):
                s = im.n * GN_STEPS
                if h == 0:
                    dve.wait_ge(x_loaded[im.p], im.pair * 16 + 16)
                    if not (isinstance(im.n, int) and im.n == 0):
                        dve.wait_ge(h32_done, im.n)
                        dve.wait_ge(h_head_done, im.n)
                nc.vector.bn_stats(stats[:, h, :], x_raw[:, h * HALF:(h + 1) * HALF]).then_inc(gn_dve, 1)
                if h == 1:
                    dve.wait_ge(gn_dve, s + 2)
                    dve.sem_inc(waited_dve, 1)
                    nc.vector.bn_aggr(mv[:, :], stats[:, :, :]).then_inc(gn_dve, 1)

            def gn_second(im, step):
                s = im.n * GN_STEPS
                if step == 0:
                    dve.wait_ge(gn_dve, s + 3)
                    dve.wait_ge(gn_pe, im.n * 2 + 1)
                    op = nc.vector.tensor_copy(gs[:, 0:1], side[1][:, 0:1])
                elif step == 1:
                    dve.wait_ge(gn_dve, s + 4)
                    op = nc.vector.tensor_tensor(gs[:, 1:2], mv[:, 0:1], gs[:, 0:1], ALU.subtract)
                else:
                    dve.wait_ge(gn_dve, s + 5)
                    op = nc.vector.tensor_scalar(gs[:, 2:3], gs[:, 1:2], gs[:, 1:2], mv[:, 1:2],
                                                 ALU.mult, ALU.add)
                op.then_inc(gn_dve, 1)

            def gn_third(im):
                dve.wait_ge(gn_pe, im.n * 2 + 2)
                nc.vector.tensor_scalar(gs[:, 6:7], side[1][:, 1:2], EPS, 1.0, ALU.add,
                                        ALU.mult).then_inc(gn_dve, 1)

            def gn_fourth(im, step):
                s = im.n * GN_STEPS
                if step == 0:
                    dve.wait_ge(gn_root, im.n + 1)
                    op = nc.vector.tensor_tensor(gs[:, 4:5], gs[:, 3:4], gnw[:, :], ALU.mult)
                elif step == 1:
                    dve.wait_ge(gn_dve, s + 8)
                    op = nc.vector.tensor_tensor(gs[:, 7:8], gs[:, 0:1], gs[:, 4:5], ALU.mult)
                else:
                    dve.wait_ge(gn_dve, s + 9)
                    op = nc.vector.tensor_tensor(gs[:, 5:6], gnb[:, 0:1], gs[:, 7:8], ALU.subtract)
                op.then_inc(gn_dve, 1)

            def qk1_tail_out(im, h):
                cols = slice(h * HALF, (h + 1) * HALF)
                dve.wait_ge(qk1_headed, im.n * 6 + h * 3 + 3)
                nc.vector.scalar_tensor_tensor(out=qk1[64:96, im.p, Q_SIDE, cols], in0=side[0][0:32, :],
                                               scalar=b1_qk[0:32, 0:1], in1=qk1[0:32, im.p, Q_SIDE, cols],
                                               op0=ALU.add, op1=ALU.subtract)
                nc.vector.scalar_tensor_tensor(out=qk1[32:64, im.p, K_SIDE, cols],
                                               in0=side[0][64:96, :], scalar=b1_qk[64:96, 0:1],
                                               in1=qk1[64:96, im.p, K_SIDE, cols], op0=ALU.add,
                                               op1=ALU.subtract).then_inc(qk1_tailed, 1)

            def v_tail_out(im, h):
                dve.wait_ge(v_headed, im.n * 2 + h + 1)
                part = (slice(None), slice(PER_HALF * h, PER_HALF * (h + 1)), slice(None))
                nc.vector.scalar_tensor_tensor(out=v_tail[part],
                                               in0=side[0][:, :].rearrange("p (t c) -> p t c", c=C),
                                               scalar=1.0 / W_UP, in1=v_head[part], op0=ALU.mult,
                                               op1=ALU.subtract).then_inc(v_tailed, 1)

            def v1_tail_out(im, h):
                dve.wait_ge(v1_headed, im.n * 2 + h + 1)
                part = (slice(None), slice(PER_HALF * h, PER_HALF * (h + 1)), slice(None))
                nc.vector.tensor_tensor(v1_tail[part], side[1][:, :].rearrange("p (t c) -> p t c", c=C),
                                        v1_head[part], ALU.subtract).then_inc(v1_tailed, 1)

            def x1_out(im, h):
                cols = slice(h * HALF, (h + 1) * HALF)
                dve.wait_ge(attended[0], im.n * 2 + h + 1)
                dve.wait_ge(x_biased, im.n + 1)
                if not (isinstance(im.n, int) and im.n < 2):
                    dve.wait_ge(y_done, (im.n - 2) * 2 + h + 1)
                nc.vector.scalar_tensor_tensor(out=x1[:, im.p, cols], in0=side[0][:, :], scalar=1.0 / P_UP,
                                               in1=xb[:, im.p, cols], op0=ALU.mult,
                                               op1=ALU.add).then_inc(x1_done, 1)

            gn_first(Image(0, 0), 0)
            gn_first(Image(0, 0), 1)
            for step in range(3):
                gn_second(Image(0, 0), step)
            gn_third(Image(0, 0))
            dve.wait_ge(gn_loaded, 32)
            for step in range(3):
                gn_fourth(Image(0, 0), step)
            dve.wait_ge(setup_loaded, 16 * N_LOADS)
            for j in range(2):
                dve.wait_ge(setup_pe, 4)
                nc.vector.tensor_scalar(w_head[:, j, :], scores[0][:, j * C:(j + 1) * C], W_UP, 1.0,
                                        ALU.mult, ALU.mult).then_inc(setup_dve, 1)
                dve.wait_ge(setup_dve, 2 * j + 1)
                nc.vector.scalar_tensor_tensor(out=w_tail[:, j, :], in0=scores[0][:, j * C:(j + 1) * C],
                                               scalar=W_UP, in1=w_head[:, j, :], op0=ALU.mult,
                                               op1=ALU.subtract).then_inc(setup_dve, 1)
            nc.vector.tensor_scalar(b_q[:, :], b_q[:, :], C ** -0.5, 1.0, ALU.mult, ALU.mult).then_inc(setup_dve, 1)
            nc.vector.tensor_copy(w_vproj_t[:, :], scores[0][:, 2 * C:3 * C]).then_inc(setup_dve, 1)
            nc.vector.tensor_copy(w1_v_t[:, :], scores[0][:, 3 * C:4 * C]).then_inc(setup_dve, 1)
            dve.wait_ge(setup_pe, 5)
            dve.wait_ge(consts_made, 1)
            for r, s in ((0, 0), (32, 0), (64, 1)):
                nc.vector.tensor_copy(w1_qk_t[:, r:r + CQK],
                                      scores[1][:, s * CQK:(s + 1) * CQK]).then_inc(setup_dve, 1)
            dve.wait_ge(setup_pe, 6)
            nc.vector.tensor_scalar(w_head[:, 2, :], scores[1][:, 2 * C:3 * C], W_UP, 1.0,
                                    ALU.mult, ALU.mult).then_inc(setup_dve, 1)
            dve.wait_ge(setup_dve, 11)
            nc.vector.scalar_tensor_tensor(out=w_tail[:, 2, :], in0=scores[1][:, 2 * C:3 * C],
                                           scalar=W_UP, in1=w_head[:, 2, :], op0=ALU.mult,
                                           op1=ALU.subtract).then_inc(setup_dve, 1)
            dve.wait_ge(setup_pe, 7)
            nc.vector.tensor_tensor(bias0[:, :], scores[1][:, C:C + 1], b_proj[:, :], ALU.add).then_inc(setup_dve, 1)
            nc.vector.tensor_scalar(gam_down[:, :], gam[:, :], 1.0 / P_UP, 1.0, ALU.mult, ALU.mult).then_inc(setup_dve, 1)
            nc.vector.tensor_tensor(gam_bv[:, :], gam[:, :], b1_v[:, :], ALU.mult).then_inc(setup_dve, 1)

            def extra(it, k, place):
                nxt, l0, l1 = it.before(-1), it.before(1), it.before(2)
                if k == 1 and not skip(l1):
                    v1_tail_out(l1, place)
                if k == 7 and last(it):
                    v1_tail_out(l0, place)
                if (k, place) in V_PLACES and not skip(it):
                    v_tail_out(it, V_PLACES.index((k, place)))

            def gn_step(it, k, step):
                if k == 2 and not skip(it.before(-1)):
                    gn_second(it.before(-1), step)
                if k == 3 and not skip(it.before(-1)):
                    gn_fourth(it.before(-1), step)

            def body(it):
                nxt, l0 = it.before(-1), it.before(1)
                for k in range(8):
                    row_max(0, it, k)
                    pt_tail_out(0, it, k, 0)
                    gn_step(it, k, 0)
                    row_max(1, it, k)
                    gn_step(it, k, 1)
                    pt_tail_out(1, it, k, 0)
                    gn_step(it, k, 2)
                    extra(it, k, 0)
                    invert(0, it, k)
                    pt_tail_out(0, it, k, 1)
                    if k in (0, 3) and not skip(l0):
                        qk1_tail_out(l0, k // 3)
                    invert(1, it, k)
                    extra(it, k, 1)
                    if k == 2 and not skip(l0):
                        x1_out(l0, 1)
                    if k == 6 and not skip(it):
                        x1_out(it, 0)
                    pt_tail_out(1, it, k, 1)
                    if k in (5, 7) and not skip(it.before(-2)):
                        gn_first(it.before(-2), k // 6)
                    if k == 2 and not skip(nxt):
                        gn_third(nxt)
                    if k == 0 and isinstance(it.n, int) and it.n == 0:
                        gn_first(nxt, 0)
                        gn_first(nxt, 1)

            for j in range(4):
                s, h = (K_SIDE, K_SIDE, Q_SIDE, Q_SIDE)[j], j % 2
                part = (slice(None), 0, s, slice(h * HALF, (h + 1) * HALF))
                dve.wait_ge(qk_headed, j + 1)
                nc.vector.tensor_tensor(qk_tail[part], qk32[:, s, h, :], qk_head[part],
                                        ALU.subtract).then_inc(qk_tailed, 1)
            every_iteration(dve, body)
            end = Image(IMAGES // 2, 1)
            for h in range(2):
                for lane in range(2):
                    pt_tail_out(lane, end, 0, h)

        @block.tensor
        def _(pe):
            mm = nc.tensor.matmul

            def split_product(dst, a_head, a_tail, b_head, b_tail, start=True, stop=True):
                mm(dst, a_head, b_head, start=start, stop=False)
                mm(dst, a_head, b_tail, start=False, stop=False)
                return mm(dst, a_tail, b_head, start=False, stop=stop)

            def score(layer, it, k):
                im, t = tile_of(layer, it, k)
                if no_tile(layer, im, t):
                    return
                first = isinstance(im.n, int) and im.n * TILES + t == 0
                if not first:
                    pe.wait_ge(exped[layer], im.n * TILES + t)
                rows = slice(t * C, (t + 1) * C)
                if layer == 0 and last(im):
                    im, rows = im.before(1), slice((t + PER_HALF) * C, (t + PER_HALF + 1) * C)
                    layer_1 = True
                else:
                    layer_1 = layer == 1
                if not layer_1:
                    if t in (0, 4):
                        pe.wait_ge(qk_tailed, im.n * 4 + (3 if t == 0 else 4))
                    for h in range(2):
                        cols = slice(h * HALF, (h + 1) * HALF)
                        done = split_product(scores[0][:, cols],
                                             qk_head[:, im.p, Q_SIDE, rows], qk_tail[:, im.p, Q_SIDE, rows],
                                             qk_head[:, im.p, K_SIDE, cols], qk_tail[:, im.p, K_SIDE, cols])
                else:
                    if t == 0:
                        pe.wait_ge(qk1_tailed, im.n * 2 + 2)
                    for h in range(2):
                        cols = slice(h * HALF, (h + 1) * HALF)
                        done = mm(scores[layer][:, cols], qk1[0:STACK, im.p, Q_SIDE, rows],
                                  qk1[0:STACK, im.p, K_SIDE, cols], start=True, stop=True)
                done.then_inc(scored[layer], 1)

            def transpose_half(layer, it, k, h):
                im, t = previous_tile(layer, it, k)
                if no_tile(layer, im, t):
                    return
                if h == 0:
                    pe.wait_ge(normed[layer], im.n * TILES + t + 1)
                if not (isinstance(im.n, int) and im.n * 16 + t * 2 + h == 0):
                    pe.wait_ge(pt_tailed[layer], im.n * 16 + t * 2 + h)
                for j in range(PER_HALF):
                    m = (PER_HALF * h + j) * C
                    done = nc.tensor.transpose(turned[layer][:, j * C:(j + 1) * C],
                                               prob[layer][:, t % 2, m:m + C], ident[:, :])
                done.then_inc(transposed[layer], 1)

            def attend(layer, im, h, t):
                if skip(im):
                    return
                if t == 0:
                    pe.wait_ge(pt_tailed[layer], im.n * 16 + 8 * (h + 1))
                    if layer == 0:
                        pe.wait_ge(v_tailed, im.n * 2 + 2)
                        if h == 1:
                            pe.wait_ge(qk1_tailed, im.n * 2 + 1)
                    else:
                        pe.wait_ge(v1_tailed, im.n * 2 + 2)
                        ahead = im.before(-3)
                        if h == 0 and not skip(ahead):
                            pe.wait_ge(gn_dve, ahead.n * GN_STEPS + 7)
                        elif h == 1 and not skip(ahead):
                            pe.wait_ge(qk_out, ahead.n * 4 + 3)
                        elif h == 1:
                            pe.wait_ge(y_scaled, im.n * 2 + 1)
                head, tail = (v_head, v_tail) if layer == 0 else (v1_head, v1_tail)
                done = split_product(side[layer][:, :], head[:, t, :], tail[:, t, :],
                                     pt_head[layer][:, h, t, :], pt_tail[layer][:, h, t, :],
                                     start=(t == 0), stop=(t == TILES - 1))
                if t == TILES - 1:
                    done.then_inc(attended[layer], 1)

            def qk_project(im, j):
                s, h = (K_SIDE, K_SIDE, Q_SIDE, Q_SIDE)[j], j % 2
                first = isinstance(im.n, int) and im.n == 0
                if first and j >= 2:
                    pe.wait_ge(qk_out, j - 1)
                elif first and j == 1:
                    pass
                elif j == 0:
                    pe.wait_ge(h_tail_done, im.n + 1)
                    pe.wait_ge(h_head_done, im.n + 1)
                    if not skip(im.before(3)):
                        pe.wait_ge(y_scaled, im.n * 2 - 5)
                elif j == 3:
                    pe.wait_ge(x1_done, im.n * 2 - 1)
                else:
                    pe.wait_ge(qk_out, im.n * 4 + j)
                cols = slice(h * HALF, (h + 1) * HALF)
                split_product(side[qk_bank(im, j)][:, :], w_head[:, s, :], w_tail[:, s, :],
                              h_head[:, im.p, cols], h_tail[:, im.p, cols]).then_inc(qk_made, 1)

            def v_project(im, h):
                if h == 0:
                    if not skip(im.before(1)):
                        pe.wait_ge(qk1_tailed, im.n * 2)
                    elif isinstance(im.n, int):
                        pe.wait_ge(setup_dve, SETUP_DVE_ALL)
                        pe.wait_ge(qk_out, 4)
                else:
                    pe.wait_ge(v_tailed, im.n * 2 + 1)
                for j in range(PER_HALF):
                    rows = slice((PER_HALF * h + j) * C, (PER_HALF * h + j + 1) * C)
                    done = split_product(side[0][:, j * C:(j + 1) * C], h_head[:, im.p, rows],
                                         h_tail[:, im.p, rows],
                                         w_head[:, 2, :], w_tail[:, 2, :])
                done.then_inc(v_made, 1)

            def qk1_project(im, h):
                pe.wait_ge(x1_done, im.n * 2 + h + 1)
                if h == 0 and not skip(im.before(-1)):
                    pe.wait_ge(qk_out, im.n * 4 + 8)
                mm(side[0][0:STACK, :], w1_qk_t[:, :], x1[:, im.p, h * HALF:(h + 1) * HALF],
                   start=True, stop=True).then_inc(qk1_made, 1)

            def v1_project(im, h):
                if h == 0:
                    if not skip(im.before(1)):
                        pe.wait_ge(y_scaled, im.n * 2)
                else:
                    pe.wait_ge(v1_tailed, im.n * 2 + 1)
                for j in range(PER_HALF):
                    rows = slice((PER_HALF * h + j) * C, (PER_HALF * h + j + 1) * C)
                    done = mm(side[1][:, j * C:(j + 1) * C], x1[:, im.p, rows], w1_v_t[:, :],
                              start=True, stop=True)
                done.then_inc(v1_made, 1)

            def gn_product(im, step):
                if step == 0:
                    if not skip(im.before(3)):
                        pe.wait_ge(v1_tailed, im.n * 2 - 4)
                    pe.wait_ge(gn_dve, im.n * GN_STEPS + 3)
                    src = mv[:, 0:1]
                else:
                    pe.wait_ge(gn_dve, im.n * GN_STEPS + 6)
                    src = gs[:, 2:3]
                mm(side[1][:, step:step + 1], group_mean[:, :], src, start=True,
                   stop=True).then_inc(gn_pe, 1)

            pe.wait_ge(consts_made, 7)
            gn_product(Image(0, 0), 0)
            gn_product(Image(0, 0), 1)
            pe.wait_ge(setup_loaded, 16 * N_LOADS)
            for j in range(2):
                nc.tensor.transpose(scores[0][:, j * C:(j + 1) * C], w_qkv[:, j, :], ident[:, :]).then_inc(setup_pe, 1)
            nc.tensor.transpose(scores[0][:, 2 * C:3 * C], w_proj[:, :], ident[:, :]).then_inc(setup_pe, 1)
            nc.tensor.transpose(scores[0][:, 3 * C:4 * C], w1_v[:, :], ident[:, :]).then_inc(setup_pe, 1)
            nc.tensor.transpose(scores[1][:, 0:2 * CQK], w1_qk[:, :],
                                ident[0:2 * CQK, 0:2 * CQK]).then_inc(setup_pe, 1)
            pe.wait_ge(setup_dve, 10)
            mm(scores[1][:, 2 * C:3 * C], w_qkv[:, 2, :], w_vproj_t[:, :], start=True, stop=True).then_inc(setup_pe, 1)
            pe.wait_ge(setup_dve, 12)
            mm(scores[1][:, C:C + 1], w_vproj_t[:, :], b_v[:, :], start=True, stop=True).then_inc(setup_pe, 1)
            pe.wait_ge(setup_dve, SETUP_DVE_ALL)
            for j in range(4):
                qk_project(Image(0, 0), j)

            def extra(it, k, place):
                nxt, l0, l1 = it.before(-1), it.before(1), it.before(2)
                if (k, place) == (7, 1) and not skip(it):
                    qk1_project(it, 0)
                if (k, place) == (3, 0) and not skip(l0):
                    qk1_project(l0, 1)
                if k == 1 and not skip(l1):
                    v1_project(l1, place)
                if k == 7 and last(it):
                    v1_project(l0, place)
                if k == 2 and not skip(nxt):
                    gn_product(nxt, place)
                if (k, place) in V_PLACES and not skip(it):
                    v_project(it, V_PLACES.index((k, place)))
                if (k, place) in QK_PLACES and not skip(nxt):
                    qk_project(nxt, QK_PLACES.index((k, place)))

            def body(it):
                l0, l1 = it.before(1), it.before(2)
                attends = {0: (1, it.before(3), 1, 4), 1: (0, l0, 1, 0), 2: (0, l0, 1, 4),
                           3: (1, l1, 0, 0), 4: (1, l1, 0, 4), 5: (0, it, 0, 0), 6: (0, it, 0, 4),
                           7: (1, l1, 1, 0)}
                if last(it):
                    attends.update({5: (1, l1, 1, 0), 6: (1, l1, 1, 4), 7: (0, it, 0, 0)})
                for k in range(8):
                    layer, im, h, t = attends[k]
                    score(0, it, k)
                    transpose_half(0, it, k, 0)
                    attend(layer, im, h, t)
                    extra(it, k, 0)
                    score(1, it, k)
                    transpose_half(1, it, k, 0)
                    attend(layer, im, h, t + 1)
                    transpose_half(0, it, k, 1)
                    attend(layer, im, h, t + 2)
                    attend(layer, im, h, t + 3)
                    transpose_half(1, it, k, 1)
                    extra(it, k, 1)

            every_iteration(pe, body)
            end = Image(IMAGES // 2, 1)
            for h in range(2):
                for lane in range(2):
                    transpose_half(lane, end, 0, h)
            for t in range(TILES):
                attend(1, end.before(2), 0, t)
            pe.wait_ge(pt_tailed[0], IMAGES * 16 + 8)
            pe.wait_ge(qk1_tailed, IMAGES * 2)
            for t in range(TILES):
                done = split_product(side[0][:, :], v1_head[:, t, :], v1_tail[:, t, :],
                                     pt_head[0][:, 0, t, :], pt_tail[0][:, 0, t, :],
                                     start=(t == 0), stop=(t == TILES - 1))
            done.then_inc(attended[0], 1)


_INS = ['x', 'L0_conv_gn_w', 'L0_conv_gn_b', 'L0_conv_qkv_w', 'L0_conv_qkv_b', 'L0_conv_proj_w',
        'L0_conv_proj_b', 'L1_conv_Wq', 'L1_conv_bq', 'L1_conv_Wk', 'L1_conv_bk', 'L1_conv_Wv',
        'L1_conv_bv', 'L1_conv_gamma']


def kernel(**inputs):
    import numpy as _np
    import concourse.bacc as _bacc
    from concourse import mybir as _mybir
    from concourse.bass_utils import run_bass_kernel_spmd as _run

    nc = _bacc.Bacc("TRN2", target_bir_lowering=False, num_devices=1)
    arrays, args = {}, []
    for name in _INS:
        a = _np.ascontiguousarray(inputs[name])
        arrays[f"in_{name}_dram"] = a
        args.append(nc.dram_tensor(f"in_{name}_dram", a.shape, _mybir.dt.from_np(a.dtype), kind="ExternalInput").ap())
    out = nc.dram_tensor("out_dram", inputs['x'].shape, _mybir.dt.float32, kind="ExternalOutput").ap()
    build(nc, *args, out)
    r = _run(nc, [arrays], core_ids=[0])
    return r.results[0]["out_dram"]
```
